# Optimizing a Trainium2 kernel written in Bass

```python
import numpy as np
import jax
import jax.numpy as jnp

def _softmax(x, axis=-1):
    return jax.nn.softmax(x, axis=axis)

def _gelu(x):
    return jax.nn.gelu(x, approximate=True)

def _silu(x):
    return jax.nn.silu(x)

def _sigmoid(x):
    return jax.nn.sigmoid(x)

def _layernorm(x, axis=-1, eps=1e-05):
    m = jnp.mean(x, axis=axis, keepdims=True)
    v = jnp.var(x, axis=axis, keepdims=True)
    return (x - m) / jnp.sqrt(v + eps)

def _scatter_add(tgt, idx, src, axis=0):
    return tgt.at[idx].add(src)

def _segment_sum(src, seg, n):
    return jax.ops.segment_sum(src, seg, n)
kernel_name = 'mk_xattn_ffn_d1_seqx_r4_9cdcb7'

def setup_inputs(seed: int=0):
    np.random.seed(seed)
    _w = jnp.asarray

    def _rec_inputs():
        import jax
        import jax.numpy as jnp
        _rk = jax.random.key(seed)
        x = -0.0003929 + 0.9999 * jax.random.normal(jax.random.fold_in(_rk, 1), (16, 128, 1024), jnp.float32)
        _lenS = 128 - jax.random.randint(jax.random.fold_in(_rk, 7), (16,), 0, max(1, 128 // 4) + 1, jnp.int32)
        _lenS2 = 128 - jax.random.randint(jax.random.fold_in(_rk, 8), (16,), 0, max(1, 128 // 4) + 1, jnp.int32)
        _ctx_4096P = jax.random.normal(jax.random.fold_in(_rk, 11), (16, 16, 1024), jnp.float32)
        _ctx_4096c = jax.random.dirichlet(jax.random.fold_in(_rk, 511), 0.3 * jnp.ones((16,), jnp.float32), (16, 128))
        _ctx_4096t = jnp.einsum('bsk,bkd->bsd', _ctx_4096c, _ctx_4096P)
        _ctx_4096t = _ctx_4096t * jax.lax.rsqrt(jnp.mean(jnp.square(_ctx_4096t)) + 1e-12) * 0.953939
        ctx_4096 = 2.81802e-05 + 1.00001 * (_ctx_4096t + 0.3 * jax.random.normal(jax.random.fold_in(_rk, 611), (16, 128, 1024), jnp.float32))
        return (x, ctx_4096)
    x, ctx_4096 = _rec_inputs()

    def _L0_xattn_setup():
        import jax, jax.numpy as jnp
        import numpy as np
        EMB_DIM = 128
        HEADS = 8
        key = jax.random.key(seed)
        kq, kk, kv = jax.random.split(key, 3)
        B, C, N = (8, EMB_DIM, 1024)
        q = jax.random.normal(kq, (B, C, N), dtype=jnp.float32)
        k = jax.random.normal(kk, (B, C, N), dtype=jnp.float32)
        v = jax.random.normal(kv, (B, C, N), dtype=jnp.float32)
        return {'q': q, 'k': k, 'v': v}
    _L0_xattn_all = _L0_xattn_setup()
    _L0_xattn_in = {k: v for k, v in _L0_xattn_all.items() if k in ()}
    del _L0_xattn_all

    def _L0_ffn_setup():
        import jax, jax.numpy as jnp
        import numpy as np
        NF4 = jnp.array([-1.0, -0.6961928009986877, -0.5250730514526367, -0.39491748809814453, -0.28444138169288635, -0.18477343022823334, -0.09105003625154495, 0.0, 0.07958029955625534, 0.16093020141124725, 0.24611230194568634, 0.33791524171829224, 0.44070982933044434, 0.5626170039176941, 0.7229568362236023, 1.0], dtype=jnp.float32)
        BLOCK = 64

        def dequant_nf4(codes, scales):
            out_dim, in_dim = codes.shape
            vals = NF4[codes].reshape(out_dim, in_dim // BLOCK, BLOCK)
            return (vals * scales[:, :, None]).reshape(out_dim, in_dim)
        key = jax.random.key(seed)
        ks = jax.random.split(key, 7)
        H, I = (1024, 2752)
        B, S = (4, 512)
        return {'x': jax.random.normal(ks[0], (B, S, H), dtype=jnp.float32), 'gate_codes': jax.random.randint(ks[1], (I, H), 0, 16, dtype=jnp.int32), 'gate_scales': jax.random.uniform(ks[2], (I, H // BLOCK), dtype=jnp.float32) * 0.02, 'up_codes': jax.random.randint(ks[3], (I, H), 0, 16, dtype=jnp.int32), 'up_scales': jax.random.uniform(ks[4], (I, H // BLOCK), dtype=jnp.float32) * 0.02, 'down_codes': jax.random.randint(ks[5], (H, I), 0, 16, dtype=jnp.int32), 'down_scales': jax.random.uniform(ks[6], (H, I // BLOCK), dtype=jnp.float32) * 0.02}
    _L0_ffn_all = _L0_ffn_setup()
    _L0_ffn_in = {k: v for k, v in _L0_ffn_all.items() if k in ('gate_codes', 'gate_scales', 'up_codes', 'up_scales', 'down_codes', 'down_scales')}
    del _L0_ffn_all
    return {'x': x, 'ctx_4096': ctx_4096, 'L0_ffn_gate_codes': _L0_ffn_in['gate_codes'], 'L0_ffn_gate_scales': _L0_ffn_in['gate_scales'], 'L0_ffn_up_codes': _L0_ffn_in['up_codes'], 'L0_ffn_up_scales': _L0_ffn_in['up_scales'], 'L0_ffn_down_codes': _L0_ffn_in['down_codes'], 'L0_ffn_down_scales': _L0_ffn_in['down_scales']}

def reference(x, ctx_4096, L0_ffn_gate_codes, L0_ffn_gate_scales, L0_ffn_up_codes, L0_ffn_up_scales, L0_ffn_down_codes, L0_ffn_down_scales):
    import jax
    import jax.numpy as jnp

    def _L0_xattn_ref(q, k, v):
        import jax, jax.numpy as jnp
        import numpy as np
        EMB_DIM = 128
        HEADS = 8
        B, C, N = q.shape
        H = HEADS
        dh = C // H
        qh = q.transpose(0, 2, 1).reshape(B, N, H, dh)
        kh = k.transpose(0, 2, 1).reshape(B, N, H, dh)
        vh = v.transpose(0, 2, 1).reshape(B, N, H, dh)
        qh = jax.nn.softmax(qh, axis=3)
        kh = jax.nn.softmax(kh, axis=1)
        kvs = jnp.einsum('bnhd,bnhe->bhde', kh, vh)
        out = jnp.einsum('bnhd,bhde->bnhe', qh, kvs)
        return out.transpose(0, 2, 3, 1).reshape(B, C, N)

    def _L0_ffn_ref(x, gate_codes, gate_scales, up_codes, up_scales, down_codes, down_scales):
        import jax, jax.numpy as jnp
        import numpy as np
        NF4 = jnp.array([-1.0, -0.6961928009986877, -0.5250730514526367, -0.39491748809814453, -0.28444138169288635, -0.18477343022823334, -0.09105003625154495, 0.0, 0.07958029955625534, 0.16093020141124725, 0.24611230194568634, 0.33791524171829224, 0.44070982933044434, 0.5626170039176941, 0.7229568362236023, 1.0], dtype=jnp.float32)
        BLOCK = 64

        def dequant_nf4(codes, scales):
            out_dim, in_dim = codes.shape
            vals = NF4[codes].reshape(out_dim, in_dim // BLOCK, BLOCK)
            return (vals * scales[:, :, None]).reshape(out_dim, in_dim)
        Wg = dequant_nf4(gate_codes, gate_scales)
        Wu = dequant_nf4(up_codes, up_scales)
        Wd = dequant_nf4(down_codes, down_scales)
        gate = jnp.einsum('bsh,ih->bsi', x, Wg)
        up = jnp.einsum('bsh,ih->bsi', x, Wu)
        inter = jax.nn.silu(gate) * up
        return jnp.einsum('bsi,hi->bsh', inter, Wd)
    x = x + _L0_xattn_ref(_layernorm(x, axis=-1), ctx_4096, ctx_4096)
    x = x + _L0_ffn_ref(_layernorm(x, axis=-1), L0_ffn_gate_codes, L0_ffn_gate_scales, L0_ffn_up_codes, L0_ffn_up_scales, L0_ffn_down_codes, L0_ffn_down_scales)
    return x

_drawn_inputs = setup_inputs


def setup_inputs(seed=0):
    import zlib

    import numpy as np

    out = dict(_drawn_inputs(seed))
    spreads = {}
    factors = {'L0_ffn_gate_scales': 8.0, 'L0_ffn_up_scales': 8.0, 'L0_ffn_down_scales': 8.0}
    for name, (base, spread) in spreads.items():
        noise = np.random.default_rng([zlib.crc32(name.encode()), seed]).standard_normal(out[name].shape)
        drawn = base * np.exp(spread * noise) if base else spread * noise
        out[name] = jnp.asarray(drawn.astype(out[name].dtype))
    for name, factor in factors.items():
        out[name] = (out[name] * factor).astype(out[name].dtype)
    return out
```

```python
from contextlib import ExitStack

import concourse.bass as bass
from concourse import mybir

F32 = mybir.dt.float32
F32R = mybir.dt.float32r
I32 = mybir.dt.int32
BF16 = mybir.dt.bfloat16
ALU = mybir.AluOpType
ACT = mybir.ActivationFunctionType
AX = mybir.AxisListType

P = 128
HEADS = 8
BLOCK = 64
EPS = 1e-5
WIDE = 512
XS = 2
LR = 4

LINES = [(0.30380716919898987, 1.1266502141952515), (0.1301555633544922, 0.12570476531982422),
         (0.09966795146465302, 0.014562471769750118), (0.09105003625154495, 0.0),
         (0.08134990185499191, -0.0017696022987365723), (0.09180294722318649, -0.02929653413593769),
         (0.12190717458724976, -0.16882604360580444), (0.2770431637763977, -1.2163453102111816)]
CENTRE = 7.0


class Turn:

    def __init__(self, p, k):
        self.n = p * XS + k
        self.slot = k % XS
        self.round = p + k // XS


class Steps:

    def __init__(self, sem):
        self.sem, self.base, self.local = sem, 0, 0

    def mark(self, ins):
        ins.then_inc(self.sem, 1)
        self.local += 1
        return self.base + self.local

    def enter(self, p, per, first=0):
        start = self.base + self.local - first * per
        self.base, self.local, self.start, self.per = p * per + start, 0, start, per

    def leave(self, end):
        assert self.local == self.per, (self.local, self.per)
        self.base, self.local = self.start + end * self.per, 0


def wait(eng, sem, value):
    if not (isinstance(value, int) and value <= 0):
        eng.wait_ge(sem, value)


def xattn_ffn(nc, x, ctx, gu_codes, gu_scales, d_codes, d_scales, out):
    B, C, N = x.shape
    T = B * C
    GU = gu_codes.shape[0]
    KT = d_codes.shape[0]
    HT = N // P
    TB = T // WIDE
    TT = T // P
    HALF = P // 2
    QT = WIDE // P
    FULL = KT - 1
    ITEM = HT * P
    assert C == P and ITEM == N and GU == 2 * FULL + 1 and N == 2 * WIDE and T == TB * WIDE
    assert B % XS == 0 and FULL % 2 == 1 and TB == 4
    NI = GU + KT

    x1_dram = nc.dram_tensor("x1_scratch", (B, P, N), F32).ap()
    wd_dram = nc.dram_tensor("wd_scratch", (KT, P, N), F32).ap()
    inter_dram = nc.dram_tensor("inter_scratch", (TT, P, KT, P), F32).ap()

    with ExitStack() as st:
        def sb(name, shape, dt):
            return st.enter_context(nc.sbuf_tensor(name, shape, dt))

        def sem(name):
            return st.enter_context(nc.semaphore(name))

        R1 = sb("R1", [P, 2 * HT * T], F32R)
        R2 = sb("R2", [P, 8 * ITEM], F32R)
        F = sb("F", [P, 15 * N], F32)
        ident = sb("ident", [P, P], F32)
        headmask = sb("headmask", [P, P], F32)
        headsel = sb("headsel", [P, HEADS], F32)
        halfneg = sb("halfneg", [P, 1], F32)
        one = sb("one", [P, 1], F32)
        bn = sb("bn", [P, 2, 6], F32)
        bn2 = sb("bn2", [P, 2, 6], F32)
        mv = sb("mv", [P, 2], F32)
        mv2 = sb("mv2", [P, 2], F32)
        veps = sb("veps", [P, 1], F32)
        veps2 = sb("veps2", [P, 1], F32)
        rstd = sb("rstd", [P, 1], F32)
        rstd2 = sb("rstd2", [P, 1], F32)
        nmr = sb("nmr", [P, 1], F32)
        nmr2 = sb("nmr2", [P, 1], F32)
        nkmax = sb("nkmax", [P, 1], F32)
        ksum = sb("ksum", [P, 1], F32)
        rksum = sb("rksum", [P, 1], F32)
        rden = sb("rden", [P, HT * HEADS], F32)
        kvs = sb("kvs", [P, P], F32)

        banks = [st.enter_context(nc.psum_tensor(f"bank{i}", [P, 2, WIDE], F32)) for i in range(4)]

        xh = R1[:, 0:HT * T].rearrange("p (t n) -> p t n", t=HT)
        xl = R1[:, HT * T:2 * HT * T].rearrange("p (t n) -> p t n", t=HT)
        wgu = R2[:, :].rearrange("p (s q g n) -> p s q g n", s=2, q=2, g=2)

        def f(i, n=1):
            return F[:, i * N:(i + n) * N]

        codes = [f(0).bitcast(I32), f(1).bitcast(I32)]
        scales = [f(2), f(3)]
        code7 = [f(4).bitcast(BF16)[:, s * N:(s + 1) * N] for s in range(2)]
        lines = [f(5 + i) for i in range(LR)]
        low, high = f(9), f(10)
        w = [f(11), f(12)]
        silu = [F[:, 13 * N + s * WIDE:13 * N + (s + 1) * WIDE] for s in range(2)]
        inter = [F[:, 14 * N + s * WIDE:14 * N + (s + 1) * WIDE] for s in range(2)]

        xs, cs = [f(13), f(0)], [f(14), f(1)]
        x1 = [f(2), f(3)]
        expq = [f(4), f(11)]
        expk, expkT, ctxT, softq, x2, rdenw = [f(5 + i) for i in range(6)]
        pT1, pT2, pT3 = [banks[i][:, :, :].rearrange("p a n -> p (a n)") for i in range(3)]
        pDen = banks[3][:, 0, 0:HT * HEADS]
        pKV = banks[3][:, 1, 0:P]

        HW = KT * WIDE
        IT = KT * P
        wdh = R1[:, 0:HW].rearrange("p (k n) -> p k n", k=KT)
        wdl = R1[:, HW:2 * HW].rearrange("p (k n) -> p k n", k=KT)
        ih = [R2[:, 0:IT], R1[:, 2 * HW:2 * HW + IT]]
        il = [R1[:, 2 * HW + IT:2 * HW + 2 * IT], R1[:, 2 * HW + 2 * IT:2 * HW + 3 * IT]]
        FS = 15
        stage = [F[:, k * WIDE:(k + 1) * WIDE] for k in range(FS)] + \
                [R2[:, IT + (k - FS) * WIDE:IT + (k - FS + 1) * WIDE].bitcast(F32) for k in range(FS, KT)]
        it = [F[:, FS * WIDE + s * IT:FS * WIDE + (s + 1) * IT] for s in range(2)]
        free = FS * WIDE + 2 * IT
        xo = [F[:, free + s * WIDE:free + (s + 1) * WIDE] for s in range(2)]
        yo = [F[:, free + (2 + s) * WIDE:free + (3 + s) * WIDE] for s in range(2)]
        assert 2 * HW + 3 * IT <= 2 * HT * T and IT + (KT - FS) * WIDE <= 8 * ITEM
        assert free >= 13 * N and free + 4 * WIDE <= 15 * N and IT <= 4 * ITEM
        GROUPS = [(0, 4), (4, 8), (8, 12), (12, FS), (FS, KT)]

        consts_ready = sem("consts_ready")
        x_in = [sem(f"x_in{s}") for s in range(XS)]
        ctx_in = [sem(f"ctx_in{s}") for s in range(XS)]
        x1_stored = [sem(f"x1_stored{s}") for s in range(XS)]
        veps_ready, rstd_ready, nmr_ready = sem("veps_ready"), sem("rstd_ready"), sem("nmr_ready")
        veps2_ready, rstd2_ready, nmr2_ready = sem("veps2_ready"), sem("rstd2_ready"), sem("nmr2_ready")
        kmax_ready, expq_ready, expk_ready = sem("kmax_ready"), sem("expq_ready"), sem("expk_ready")
        ctx_turned, ctxT_ready = sem("ctx_turned"), sem("ctxT_ready")
        expk_turned, expkT_ready = sem("expk_turned"), sem("expkT_ready")
        den_done, rden_ready, rdenw_ready = sem("den_done"), sem("rden_ready"), sem("rdenw_ready")
        rksum_ready, rden_turned = sem("rksum_ready"), sem("rden_turned")
        kv_done, kvs_ready, softq_ready = sem("kv_done"), sem("kvs_ready"), sem("softq_ready")
        attn_done, x1_ready, x2_ready = sem("attn_done"), sem("x1_ready"), sem("x2_ready")
        x2_turned, xh_ready, xl_ready = sem("x2_turned"), sem("xh_ready"), sem("xl_ready")
        codes_in = [sem(f"codes_in{s}") for s in range(2)]
        scales_in = [sem(f"scales_in{s}") for s in range(2)]
        code7_ready, line_ready, lines_merged = sem("code7_ready"), sem("line_ready"), sem("lines_merged")
        w_ready, wh_ready, wl_ready = sem("w_ready"), sem("wh_ready"), sem("wl_ready")
        wd_stored = [sem(f"wd_stored{s}") for s in range(2)]
        gate_done, up_done, silu_ready = sem("gate_done"), sem("up_done"), sem("silu_ready")
        blocks_done = sem("blocks_done")
        up_copied = sem("up_copied")
        inter_stored = [sem(f"inter_stored{s}") for s in range(2)]
        stage_in = [sem(f"stage_in{g}") for g in range(len(GROUPS))]
        wdh_ready, wdl_ready = sem("wdh_ready"), sem("wdl_ready")
        inter_in = [sem(f"inter_in{s}") for s in range(2)]
        last_in = [sem(f"last_in{s}") for s in range(2)]
        x1_in = [sem(f"x1_in{s}") for s in range(2)]
        ih_ready, il_ready = sem("ih_ready"), sem("il_ready")
        ih_first, il_first = sem("ih_first"), sem("il_first")
        down_step, y_ready = sem("down_step"), sem("y_ready")
        y_stored = [sem(f"y_stored{s}") for s in range(2)]
        dve_step = sem("dve_step")
        pool_step = sem("pool_step")

        NCONST = 3
        LOOPS = B // XS - 1
        PAIRS = FULL // 2
        TILES = 2 * TT

        def stages(p, k):
            i = p * XS + k
            if not isinstance(i, int):
                return Turn(p, k), Turn(p, k - 1), Turn(p, k - 2)
            return [Turn(p, k - d) if 0 <= i - d < B else None for d in range(3)]

        def tokens_of(v, t):
            return v[:, :, t.n * P:(t.n + 1) * P] if isinstance(t.n, int) else v[:, :, bass.ds(t.n * P, P)]

        block = st.enter_context(nc.Block())

        @block.sync
        def _(sp):
            def load_codes(n, slot, src):
                sp.dma_start(codes[slot], src).then_inc(codes_in[slot], 16)

            def load_scales(n, slot, src):
                sp.dma_start(scales[slot], src.unsqueeze(1).to_broadcast([2, BLOCK, ITEM])).then_inc(scales_in[slot], 16)

            def at(a, i):
                return a[i] if isinstance(i, int) else a[bass.ds(i, 1)].rearrange("o p n -> (o p) n")

            def load_item(n, slot, cod, scl, i):
                wait(sp, code7_ready, n - 1)
                load_codes(n, slot, at(cod, i))
                wait(sp, w_ready, n - 1)
                load_scales(n, slot, at(scl, i))

            def load_x(t):
                sp.dma_start(xs[t.slot], at(x, t.n)).then_inc(x_in[t.slot], 16)

            def load_ctx(t):
                sp.dma_start(cs[t.slot], at(ctx, t.n)).then_inc(ctx_in[t.slot], 16)

            load_item(0, 0, gu_codes, gu_scales, 0)
            load_item(1, 1, gu_codes, gu_scales, 1)
            load_x(Turn(0, 0))
            load_ctx(Turn(0, 0))
            sp.wait_ge(wl_ready, 2)
            load_x(Turn(0, 1))
            load_ctx(Turn(0, 1))

            def mixer_turn(p, k, load):
                b, new = Turn(p, k - 1), Turn(p, k + 1)
                if stages(p, k)[2]:
                    c = Turn(p, k - 2)
                    sp.wait_ge(x1_stored[c.slot], (c.round + 1) * 16)
                if load:
                    sp.wait_ge(ctx_turned, b.n + 1)
                    sp.wait_ge(expk_ready, b.n + 1)
                    load_ctx(new)
                sp.wait_ge(x1_ready, b.n + 1)
                if load:
                    load_x(new)
                sp.dma_start(at(x1_dram, b.n), x1[b.slot]).then_inc(x1_stored[b.slot], 16)

            mixer_turn(0, 1, True)
            with sp.Fori(0, LOOPS - 1) as p:
                for k in range(2, 2 + XS):
                    mixer_turn(p, k, True)
            for k in range(2, 2 + XS + 1):
                mixer_turn(LOOPS - 1, k, k == 2)

            sp.wait_ge(xl_ready, B)
            for s in range(XS):
                sp.wait_ge(x1_stored[s], B // XS * 16)
            load_item(2, 0, d_codes, d_scales, 0)
            load_item(3, 1, gu_codes, gu_scales, 2)

            def store_block(c, tb, rows=None):
                s = tb % 2
                sp.wait_ge(blocks_done, c * TB + tb + 1 + TB)
                if rows is None:
                    dst = inter_dram[tb * QT:(tb + 1) * QT, :, bass.ds(c, 1), :].rearrange("q p o n -> p (q o) n")
                    sp.dma_start(dst, inter[s].rearrange("p (q n) -> p q n", q=QT)).then_inc(inter_stored[s], 16)
                    return
                for a in range(2):
                    dst = inter_dram[tb * QT:(tb + 1) * QT, a * HALF:(a + 1) * HALF, c, :].rearrange("q p n -> p q n")
                    sp.dma_start(dst, inter[s][0:HALF, :].rearrange("p (q n) -> p q n", q=QT)).then_inc(inter_stored[s], 16)

            def store_wd(c, par):
                sp.wait_ge(w_ready, c * 3 + 3)
                sp.dma_start(at(wd_dram, c), w[par]).then_inc(wd_stored[par], 16)

            with sp.Fori(0, PAIRS) as p:
                for j in range(2):
                    c = p * 2 + j
                    n = p * 6 + 2 + 3 * j
                    load_item(n + 2, j, gu_codes, gu_scales, c * 2 + 3)
                    store_wd(c, j)
                    store_block(c, 0)
                    load_item(n + 3, 1 - j, d_codes, d_scales, c + 1)
                    store_block(c, 1)
                    load_item(n + 4, j, gu_codes, gu_scales, c * 2 + 4)
                    store_block(c, 2)
                    store_block(c, 3)
            c = FULL - 1
            load_item(NI - 1, 0, d_codes, d_scales, KT - 1)
            store_wd(c, c % 2)
            store_block(c, 0)
            store_block(c, 1)
            sp.wait_ge(w_ready, NI)
            sp.dma_start(wd_dram[KT - 1], w[0]).then_inc(wd_stored[0], 16)
            store_block(c, 2)
            store_block(c, 3)
            sp.wait_ge(wd_stored[0], 16 * (FULL // 2 + 2))
            sp.wait_ge(wd_stored[1], 16 * (FULL // 2))

            def load_stage(half, g):
                a, b = GROUPS[g]
                src = wd_dram[a:b, :, half * WIDE:(half + 1) * WIDE].rearrange("k p n -> p k n")
                if a < FS:
                    dst = F[:, a * WIDE:b * WIDE].rearrange("p (k n) -> p k n", n=WIDE)
                else:
                    dst = R2[:, IT:IT + (b - a) * WIDE].bitcast(F32).rearrange("p (k n) -> p k n", n=WIDE)
                sp.dma_start(dst, src).then_inc(stage_in[g], 16)

            def load_tile(t, slot, half, cols=(0, KT)):
                g = t + half * TT
                wait(sp, il_ready, g - 1)
                a, b = cols
                dst = it[slot][:, a * P:b * P].rearrange("p (k n) -> p k n", n=P)
                src = inter_dram[t] if isinstance(t, int) else \
                    inter_dram[bass.ds(t, 1)].rearrange("o p k n -> (o p) k n")
                sp.dma_start(dst, src[:, a:b, :]).then_inc(inter_in[slot], 16)

            for s in range(2):
                sp.wait_ge(inter_stored[s], 16 * 2 * FULL)
            load_tile(0, 0, 0, (0, FULL))
            for g in range(len(GROUPS) - 1):
                load_stage(0, g)
            load_tile(1, 1, 0, (0, FULL))
            for tb in range(TB):
                store_block(FULL, tb, HALF)
            sp.wait_ge(gate_done, TB * KT)
            load_stage(0, len(GROUPS) - 1)
            for s in range(2):
                sp.wait_ge(inter_stored[s], 16 * (2 * FULL + 4))
            for t in range(2):
                sp.dma_start(it[t][:, FULL * P:], inter_dram[t, :, FULL, :]).then_inc(last_in[t], 16)

            def load_x1(t, slot, half):
                sp.dma_start(xo[slot], at(x1_dram, t)[:, half * WIDE:(half + 1) * WIDE]).then_inc(x1_in[slot], 16)

            def store_y(t, slot, half):
                sp.wait_ge(y_ready, t + half * TT + 1)
                sp.dma_start(at(out, t)[:, half * WIDE:(half + 1) * WIDE], yo[slot]).then_inc(y_stored[slot], 16)

            for half in range(2):
                for t in range(2):
                    if half:
                        load_tile(t, t, half)
                    if half:
                        store_y(TT - 2 + t, t, half - 1)
                    load_x1(t, t, half)
                if half == 0:
                    for g in range(len(GROUPS)):
                        sp.wait_ge(wdl_ready, GROUPS[g][1])
                        load_stage(1, g)
                with sp.Fori(0, TT // 2 - 1) as q:
                    for s in range(2):
                        t = q * 2 + 2 + s
                        load_tile(t, s, half)
                        store_y(t - 2, s, half)
                        load_x1(t, s, half)
            for s in range(2):
                store_y(TT - 2 + s, s, 1)
            for s in range(2):
                sp.wait_ge(y_stored[s], 16 * TT)

        @block.gpsimd
        def _(pool):
            own = Steps(pool_step)
            m = [own.mark(nc.gpsimd.memset(a, v)) for a, v in
                 ((ident[:, :], 0.0), (headmask[:, :], 1.0), (headsel[:, :], 1.0), (halfneg[:, :], -0.5), (one[:, :], 1.0))]
            pool.wait_ge(pool_step, m[-1])
            nc.gpsimd.affine_select(out=ident[:, :], in_=ident[:, :], compare_op=ALU.not_equal, fill=1.0, base=0,
                                    pattern=[[-1, P]], channel_multiplier=1).then_inc(consts_ready, 1)
            D = P // HEADS
            for a, cols in ((headmask[:, :].rearrange("p (h d) -> p h d", h=HEADS), D), (headsel[:, :].unsqueeze(2), 1)):
                k = own.mark(nc.gpsimd.affine_select(out=a, in_=a, compare_op=ALU.is_ge, fill=0.0, base=0,
                                                     pattern=[[-D, HEADS], [0, cols]], channel_multiplier=1))
                pool.wait_ge(pool_step, k)
                nc.gpsimd.affine_select(out=a, in_=a, compare_op=ALU.is_ge, fill=0.0, base=D - 1,
                                        pattern=[[D, HEADS], [0, cols]], channel_multiplier=-1).then_inc(consts_ready, 1)

            def power(src_ready, n, dst, src, ready):
                pool.wait_ge(src_ready, n + 1)
                nc.gpsimd.tensor_tensor(dst, src, halfneg[:, :], ALU.pow).then_inc(ready, 1)

            def mixer_turn(p, k):
                a, b, _ = stages(p, k)
                if a:
                    power(veps_ready, a.n, rstd[:, :], veps[:, :], rstd_ready)
                if b:
                    power(veps2_ready, b.n, rstd2[:, :], veps2[:, :], rstd2_ready)
                if a:
                    pool.wait_ge(rden_ready, a.n + 1)
                    wait(pool, rden_turned, a.n)
                    nc.gpsimd.tensor_tensor(rdenw.rearrange("p (t d) -> p t d", d=D),
                                            rden[:, :].unsqueeze(2).to_broadcast([P, HT * HEADS, D]),
                                            one[:, :].unsqueeze(2).to_broadcast([P, HT * HEADS, D]),
                                            ALU.mult).then_inc(rdenw_ready, 1)

            mixer_turn(0, 0)
            mixer_turn(0, 1)
            with pool.Fori(0, LOOPS) as p:
                for k in range(2, 2 + XS):
                    mixer_turn(p, k)
            mixer_turn(LOOPS, 2)
            mixer_turn(LOOPS, 3)

        def lines_of(act, n, s, middle=None):
            act.wait_ge(code7_ready, n + 1)
            for q in range(8):
                if q < LR:
                    wait(act, lines_merged, (n - 1) * 6 + [4, 4, 5, 6][q])
                else:
                    act.wait_ge(lines_merged, n * 6 + [1, 1, 2, 3][q - LR])
                slope, offset = LINES[q]
                nc.scalar.activation(lines[q % LR], code7[s], ACT.Copy, bias=offset, scale=slope).then_inc(line_ready, 1)
                if q == LR - 1 and middle:
                    middle()

        @block.scalar
        def _(act):
            def hi_of(n, s, c, g, par):
                act.wait_ge(w_ready, n + 1)
                wait(act, up_done, (c - 1) * TB)
                nc.scalar.activation(wgu[:, par, 0, g], w[s], ACT.Copy).then_inc(wh_ready, 1)

            def mixer_turn(p, k):
                a, b, c = stages(p, k)
                if a:
                    act.wait_ge(nmr_ready, a.n + 1)
                    if c:
                        act.wait_ge(softq_ready, c.n + 1)
                    nc.scalar.activation(expq[a.slot], xs[a.slot], ACT.Exp, bias=nmr[:, :], scale=rstd[:, :]).then_inc(expq_ready, 1)
                    act.wait_ge(kmax_ready, a.n + 1)
                    wait(act, expk_turned, a.n)
                    wait(act, rksum_ready, a.n)
                    nc.scalar.activation(expk, cs[a.slot], ACT.Exp, bias=nkmax[:, :], accum_out=ksum[:, :]).then_inc(expk_ready, 1)
                if c:
                    act.wait_ge(x2_turned, c.n + 1)
                    nc.scalar.copy(tokens_of(xh, c), pT2.rearrange("p (t n) -> p t n", t=HT)).then_inc(xh_ready, 1)
                if a:
                    act.wait_ge(ctx_turned, a.n + 1)
                    wait(act, kv_done, a.n)
                    nc.scalar.copy(ctxT, pT2).then_inc(ctxT_ready, 1)
                    act.wait_ge(expk_turned, a.n + 1)
                    nc.scalar.copy(expkT, pT1).then_inc(expkT_ready, 1)
                if b:
                    act.wait_ge(nmr2_ready, b.n + 1)
                    if c:
                        act.wait_ge(x2_turned, c.n + 1)
                    nc.scalar.activation(x2, x1[b.slot], ACT.Identity, bias=nmr2[:, :], scale=rstd2[:, :]).then_inc(x2_ready, 1)

            lines_of(act, 0, 0)
            hi_of(0, 0, 0, 0, 0)
            lines_of(act, 1, 1)
            hi_of(1, 1, 0, 1, 0)
            mixer_turn(0, 0)
            mixer_turn(0, 1)
            with act.Fori(0, LOOPS) as p:
                for k in range(2, 2 + XS):
                    mixer_turn(p, k)
            mixer_turn(LOOPS, 2)
            mixer_turn(LOOPS, 3)

            def silu_of(c, tb):
                act.wait_ge(gate_done, c * TB + tb + 1)
                act.wait_ge(blocks_done, c * TB + tb - 1 + TB)
                nc.scalar.activation(silu[tb % 2], banks[tb][:, 0, :], ACT.Silu).then_inc(silu_ready, 1)

            def chunk_pair(p):
                for j in range(2):
                    c = p * 2 + j
                    n = p * 6 + 2 + 3 * j
                    lines_of(act, n, j)
                    silu_of(c, 0)
                    lines_of(act, n + 1, 1 - j)
                    silu_of(c, 1)
                    lines_of(act, n + 2, j, lambda: hi_of(n + 1, 1 - j, c + 1, 0, 1 - j))
                    hi_of(n + 2, j, c + 1, 1, 1 - j)
                    silu_of(c, 2)
                    silu_of(c, 3)

            chunk_pair(0)
            with act.Fori(1, PAIRS) as p:
                chunk_pair(p)
            c = FULL - 1
            lines_of(act, NI - 3, 0)
            silu_of(c, 0)
            lines_of(act, NI - 2, 1)
            hi_of(NI - 2, 1, FULL, 0, 1)
            silu_of(c, 1)
            lines_of(act, NI - 1, 0)
            silu_of(c, 2)
            silu_of(c, 3)
            for tb in range(TB):
                s = tb % 2
                act.wait_ge(gate_done, FULL * TB + tb + 1)
                act.wait_ge(blocks_done, FULL * TB + tb - 1 + TB)
                nc.scalar.activation(silu[s][0:HALF, :], banks[tb][0:HALF, 0, :], ACT.Silu).then_inc(silu_ready, 1)
                act.wait_ge(inter_stored[s], 16 * (2 * FULL + 2 * (tb // 2)))
                nc.scalar.copy(inter[s][0:HALF, :], banks[tb][HALF:P, 0, :]).then_inc(up_copied, 1)

            def split_weights(half):
                for g, (a, b) in enumerate(GROUPS):
                    act.wait_ge(stage_in[g], 16 * (half + 1))
                    for k in range(a, b):
                        if half:
                            act.wait_ge(down_step, KT * (TT - 1) + k + 1)
                        nc.scalar.copy(wdh[:, k, :], stage[k]).then_inc(wdh_ready, 1)

            def split_tile(g, slot, uses):
                act.wait_ge(inter_in[slot], uses)
                wait(act, down_step, (g - 1) * KT)
                nc.scalar.copy(ih[slot], it[slot]).then_inc(ih_ready, 1)

            act.wait_ge(inter_in[0], 16)
            act.wait_ge(up_done, FULL * TB)
            nc.scalar.copy(ih[0][:, 0:FULL * P], it[0][:, 0:FULL * P]).then_inc(ih_first, 1)
            act.wait_ge(gate_done, TB * KT)
            split_weights(0)
            act.wait_ge(last_in[0], 16)
            nc.scalar.copy(ih[0][:, FULL * P:], it[0][:, FULL * P:]).then_inc(ih_ready, 1)
            act.wait_ge(last_in[1], 16)
            split_tile(1, 1, 16)
            for half in range(2):
                g0, u0 = half * TT, 16 * half * TT // 2
                if half:
                    split_tile(g0, 0, u0 + 16)
                    split_weights(half)
                    split_tile(g0 + 1, 1, u0 + 16)
                with act.Fori(0, TT // 2 - 1) as q:
                    for s in range(2):
                        split_tile(q * 2 + (g0 + 2 + s), s, q * 16 + (u0 + 32))

        @block.vector
        def _(dve):
            own = Steps(dve_step)

            def after(token):
                dve.wait_ge(dve_step, token)

            for i in range(TB):
                nc.vector.memset(bn[:, 0, i:i + 1], 0.0).then_inc(blocks_done, 1)

            def centre(n, s):
                dve.wait_ge(codes_in[s], centre_round(n))
                nc.vector.tensor_scalar(code7[s], codes[s], CENTRE, None, ALU.subtract).then_inc(code7_ready, 1)

            def centre_round(n):
                return 16 * (n // 2 + 1)

            def merge(n, s, round_, middle=None, w_free=None):
                at = lambda q: lines[q % LR]
                vt = nc.vector
                dve.wait_ge(line_ready, n * 8 + 2)
                vt.scalar_tensor_tensor(low, at(0), 0.0, at(1), ALU.min, ALU.min).then_inc(lines_merged, 1)
                for q in (2, 3):
                    dve.wait_ge(line_ready, n * 8 + q + 1)
                    dve.wait_ge(lines_merged, n * 6 + q - 1)
                    vt.tensor_tensor(low, low, at(q), ALU.min).then_inc(lines_merged, 1)
                if middle:
                    middle()
                dve.wait_ge(line_ready, n * 8 + 6)
                vt.tensor_tensor(high, at(4), at(5), ALU.max).then_inc(lines_merged, 1)
                for q in (6, 7):
                    dve.wait_ge(line_ready, n * 8 + q + 1)
                    dve.wait_ge(lines_merged, n * 6 + q - 2)
                    vt.tensor_tensor(high, high, at(q), ALU.max).then_inc(lines_merged, 1)
                if w_free:
                    dve.wait_ge(*w_free)
                dve.wait_ge(lines_merged, n * 6 + 6)
                after(own.mark(vt.scalar_tensor_tensor(w[s], high, 0.0, low, ALU.max, ALU.add)))
                dve.wait_ge(scales_in[s], round_)
                vt.tensor_tensor(w[s], w[s], scales[s], ALU.mult).then_inc(w_ready, 1)

            def lo_of(m, s, g, par):
                dve.wait_ge(wh_ready, m + 1)
                nc.vector.tensor_tensor(wgu[:, par, 1, g], w[s], wgu[:, par, 0, g].bitcast(F32), ALU.subtract).then_inc(wl_ready, 1)

            for n in range(2):
                centre(n, n)
                merge(n, n, 16)
                dve.wait_ge(w_ready, n + 1)
                lo_of(n, n, n, 0)

            def stats(src, bn_, mv_, veps_, ready):
                for i in range(2):
                    nc.vector.bn_stats(bn_[:, i, :], src[:, i * WIDE:(i + 1) * WIDE])
                dve.drain()
                after(own.mark(nc.vector.bn_aggr(mv_[:, :], bn_[:, :, :].rearrange("p a n -> p (a n)"))))
                nc.vector.tensor_scalar(veps_[:, :], mv_[:, 1:2], EPS, None, ALU.add).then_inc(ready, 1)

            def mixer_turn(p, k):
                a, b, c = stages(p, k)
                if a:
                    dve.wait_ge(x_in[a.slot], (a.round + 1) * 16)
                    stats(xs[a.slot], bn, mv, veps, veps_ready)
                    dve.wait_ge(ctx_in[a.slot], (a.round + 1) * 16)
                    nc.vector.tensor_reduce(nkmax[:, :], cs[a.slot], AX.X, ALU.max, negate=True).then_inc(kmax_ready, 1)
                    dve.wait_ge(rstd_ready, a.n + 1)
                    nc.vector.scalar_tensor_tensor(nmr[:, :], mv[:, 0:1], -1.0, rstd[:, :], ALU.mult, ALU.mult).then_inc(nmr_ready, 1)
                if b:
                    dve.wait_ge(kv_done, b.n + 1)
                    dve.wait_ge(rksum_ready, b.n + 1)
                    nc.vector.scalar_tensor_tensor(kvs[:, :], pKV, rksum[:, :], headmask[:, :], ALU.mult, ALU.mult).then_inc(kvs_ready, 1)
                if b:
                    dve.wait_ge(rden_turned, b.n + 1)
                    nc.vector.tensor_tensor(softq, expq[b.slot], pT3, ALU.mult).then_inc(softq_ready, 1)
                if c:
                    dve.wait_ge(xh_ready, c.n + 1)
                    h, l = (tokens_of(v, c) for v in (xh, xl))
                    nc.vector.tensor_tensor(l, pT2.rearrange("p (t n) -> p t n", t=HT), h.bitcast(F32), ALU.subtract).then_inc(xl_ready, 1)
                if b:
                    dve.wait_ge(attn_done, b.n + 1)
                    if not a:
                        dve.wait_ge(x1_stored[b.slot], b.round * 16)
                    nc.vector.tensor_tensor(x1[b.slot], xs[b.slot], pT1, ALU.add).then_inc(x1_ready, 1)
                    dve.wait_ge(x1_ready, b.n + 1)
                    stats(x1[b.slot], bn2, mv2, veps2, veps2_ready)
                if a:
                    dve.wait_ge(den_done, a.n + 1)
                    nc.vector.reciprocal(rden[:, :], pDen).then_inc(rden_ready, 1)
                    dve.wait_ge(expk_ready, a.n + 1)
                    nc.vector.reciprocal(rksum[:, :], ksum[:, :]).then_inc(rksum_ready, 1)
                if b:
                    dve.wait_ge(rstd2_ready, b.n + 1)
                    nc.vector.scalar_tensor_tensor(nmr2[:, :], mv2[:, 0:1], -1.0, rstd2[:, :], ALU.mult, ALU.mult).then_inc(nmr2_ready, 1)

            dve.wait_ge(consts_ready, NCONST)
            mixer_turn(0, 0)
            mixer_turn(0, 1)
            with dve.Fori(0, LOOPS) as p:
                own.enter(p, XS * 2)
                for k in range(2, 2 + XS):
                    mixer_turn(p, k)
            own.leave(LOOPS)
            mixer_turn(LOOPS, 2)
            mixer_turn(LOOPS, 3)

            def block_out(c, tb):
                dve.wait_ge(silu_ready, c * TB + tb + 1)
                dve.wait_ge(up_done, c * TB + tb + 1)
                wait(dve, inter_stored[tb % 2], c * 32 + 16 * (tb // 2))
                nc.vector.tensor_tensor(inter[tb % 2], silu[tb % 2], banks[tb][:, 1, :], ALU.mult).then_inc(blocks_done, 1)

            centre(2, 0)
            def chunk_pair(p):
                for j in range(2):
                    c = p * 2 + j
                    n = p * 6 + 2 + 3 * j

                    def centre_in(k, s):
                        dve.wait_ge(codes_in[s], p * 48 + 16 * (k // 2 + 1))
                        nc.vector.tensor_scalar(code7[s], codes[s], CENTRE, None, ALU.subtract).then_inc(code7_ready, 1)

                    def round_in(k):
                        return p * 48 + 16 * (k // 2 + 1)

                    k = 2 + 3 * j
                    merge(n, j, round_in(k), lambda: centre_in(k + 1, 1 - j))
                    block_out(c, 0)
                    merge(n + 1, 1 - j, round_in(k + 1), lambda: centre_in(k + 2, j))
                    block_out(c, 1)

                    def middle():
                        dve.wait_ge(w_ready, n + 2)
                        lo_of(c * 2 + 2, 1 - j, 0, 1 - j)
                        centre_in(k + 3, 1 - j)
                    merge(n + 2, j, round_in(k + 2), middle, (wd_stored[j], p * 16 + 16))
                    dve.wait_ge(w_ready, n + 3)
                    lo_of(c * 2 + 3, j, 1, 1 - j)
                    block_out(c, 2)
                    block_out(c, 3)

            chunk_pair(0)
            with dve.Fori(1, PAIRS) as p:
                own.enter(p, 6, first=1)
                chunk_pair(p)
            own.leave(PAIRS)

            c = FULL - 1

            def centre_last(n, s):
                dve.wait_ge(codes_in[s], 16 * (n // 2 + 1))
                nc.vector.tensor_scalar(code7[s], codes[s], CENTRE, None, ALU.subtract).then_inc(code7_ready, 1)

            merge(NI - 3, 0, 16 * ((NI - 3) // 2 + 1), lambda: centre_last(NI - 2, 1))
            block_out(c, 0)
            merge(NI - 2, 1, 16 * ((NI - 2) // 2 + 1), lambda: centre_last(NI - 1, 0))
            dve.wait_ge(w_ready, NI - 1)
            lo_of(2 * FULL, 1, 0, 1)
            block_out(c, 1)
            merge(NI - 1, 0, 16 * ((NI - 1) // 2 + 1), None, (wd_stored[0], 16 * (FULL // 2 + 1)))
            block_out(c, 2)
            block_out(c, 3)
            for tb in range(TB):
                s = tb % 2
                dve.wait_ge(silu_ready, FULL * TB + tb + 1)
                dve.wait_ge(up_copied, tb + 1)
                nc.vector.tensor_tensor(inter[s][0:HALF, :], inter[s][0:HALF, :], silu[s][0:HALF, :], ALU.mult).then_inc(blocks_done, 1)

            def split_weights(half):
                for k in range(KT):
                    dve.wait_ge(wdh_ready, half * KT + k + 1)
                    nc.vector.tensor_tensor(wdl[:, k, :], stage[k], wdh[:, k, :].bitcast(F32), ALU.subtract).then_inc(wdl_ready, 1)

            def lo_full(slot):
                h = ih[slot].bitcast(F32)
                return nc.vector.tensor_tensor(il[slot][:, 0:FULL * P], it[slot][:, 0:FULL * P], h[:, 0:FULL * P], ALU.subtract)

            def lo_last(slot):
                h = ih[slot].bitcast(F32)
                nc.vector.tensor_tensor(ih[slot][HALF:P, FULL * P:], it[slot][HALF:P, FULL * P:], h[HALF:P, FULL * P:],
                                        ALU.subtract).then_inc(il_ready, 1)

            def split_tile(g, slot):
                dve.wait_ge(ih_ready, g + 1)
                lo_full(slot)
                lo_last(slot)

            def tile_out(g, slot, uses):
                dve.wait_ge(down_step, (g + 1) * KT)
                dve.wait_ge(x1_in[slot], uses)
                wait(dve, y_stored[slot], uses - 16)
                nc.vector.tensor_tensor(yo[slot], xo[slot], banks[slot][:, 0, :], ALU.add).then_inc(y_ready, 1)

            for s in range(2):
                dve.wait_ge(inter_stored[s], 16 * (2 * FULL + 4))
            for half in range(2):
                g0 = half * TT
                if half:
                    split_tile(g0, 0)
                    split_weights(half)
                    tile_out(g0 - 1, 1, 16 * (TT // 2))
                else:
                    split_weights(half)
                    dve.wait_ge(ih_first, 1)
                    lo_full(0).then_inc(il_first, 1)
                    dve.wait_ge(ih_ready, 1)
                    lo_last(0)
                split_tile(g0 + 1, 1)
                tile_out(g0, 0, 16 * (half * TT // 2 + 1))
                split_tile(g0 + 2, 0)
                tile_out(g0 + 1, 1, 16 * (half * TT // 2 + 1))
                with dve.Fori(0, TT // 2 - 2) as q:
                    for s in range(2):
                        g = q * 2 + (g0 + 3 + s)
                        split_tile(g, 1 - s)
                        tile_out(g - 1, s, q * 16 + 16 * (half * TT // 2 + 2))
                split_tile(g0 + TT - 1, 1)
                tile_out(g0 + TT - 2, 0, 16 * (half + 1) * TT // 2)
            tile_out(TILES - 1, 1, 16 * TT)

        @block.tensor
        def _(pe):
            def turn_tiles(dst, src):
                for t in range(HT):
                    i = pe.transpose(dst[:, t * P:(t + 1) * P], src[:, t * P:(t + 1) * P], ident[:, :])
                return i

            def mixer_turn(p, k):
                a, b, c = stages(p, k)
                if b:
                    pe.wait_ge(ctxT_ready, b.n + 1)
                    pe.wait_ge(expkT_ready, b.n + 1)
                    for t in range(HT):
                        i = pe.matmul(pKV, expkT[:, t * P:(t + 1) * P], ctxT[:, t * P:(t + 1) * P],
                                      start=(t == 0), stop=(t == HT - 1))
                    i.then_inc(kv_done, 1)
                    pe.wait_ge(rdenw_ready, b.n + 1)
                    turn_tiles(pT3, rdenw).then_inc(rden_turned, 1)
                if c:
                    pe.wait_ge(x2_ready, c.n + 1)
                    pe.wait_ge(ctxT_ready, min(c.n + 2, B) if isinstance(c.n, int) else c.n + 2)
                    turn_tiles(pT2, x2).then_inc(x2_turned, 1)
                if a:
                    pe.wait_ge(expq_ready, a.n + 1)
                    wait(pe, rden_ready, a.n)
                    for t in range(HT):
                        i = pe.matmul(pDen[:, t * HEADS:(t + 1) * HEADS], expq[a.slot][:, t * P:(t + 1) * P], headsel[:, :],
                                      start=True, stop=True)
                    i.then_inc(den_done, 1)
                if b:
                    pe.wait_ge(kvs_ready, b.n + 1)
                    pe.wait_ge(softq_ready, b.n + 1)
                    for h in range(2):
                        i = pe.matmul(pT1[:, h * WIDE:(h + 1) * WIDE], kvs[:, :], softq[:, h * WIDE:(h + 1) * WIDE],
                                      start=True, stop=True)
                    i.then_inc(attn_done, 1)
                if a:
                    pe.wait_ge(ctx_in[a.slot], (a.round + 1) * 16)
                    if c:
                        pe.wait_ge(xl_ready, c.n + 1)
                    turn_tiles(pT2, cs[a.slot]).then_inc(ctx_turned, 1)
                    pe.wait_ge(expk_ready, a.n + 1)
                    if b:
                        pe.wait_ge(x1_ready, b.n + 1)
                    turn_tiles(pT1, expk).then_inc(expk_turned, 1)

            pe.wait_ge(consts_ready, NCONST)
            mixer_turn(0, 0)
            mixer_turn(0, 1)
            with pe.Fori(0, LOOPS) as p:
                for k in range(2, 2 + XS):
                    mixer_turn(p, k)
            mixer_turn(LOOPS, 2)
            mixer_turn(LOOPS, 3)

            def products(dst, par, g, tb):
                for t in range(HT):
                    hi, lo = (wgu[:, par, q, g, t * P:(t + 1) * P] for q in range(2))
                    cols = slice(tb * WIDE, (tb + 1) * WIDE)
                    pe.matmul(dst, hi, xh[:, t, cols], start=(t == 0), stop=False)
                    pe.matmul(dst, hi, xl[:, t, cols], start=False, stop=False)
                    i = pe.matmul(dst, lo, xh[:, t, cols], start=False, stop=(t == HT - 1))
                return i

            def chunk(c, par):
                for tb in range(TB):
                    pe.wait_ge(blocks_done, c * TB + tb + 1)
                    if tb == 0:
                        pe.wait_ge(wl_ready, c * 2 + 1)
                    products(banks[tb][:, 0, :], par, 0, tb).then_inc(gate_done, 1)
                    if tb == 0:
                        pe.wait_ge(wl_ready, c * 2 + 2)
                    products(banks[tb][:, 1, :], par, 1, tb).then_inc(up_done, 1)

            pe.wait_ge(xl_ready, B)
            with pe.Fori(0, PAIRS) as p:
                for j in range(2):
                    chunk(p * 2 + j, j)
            chunk(FULL - 1, 0)
            for tb in range(TB):
                pe.wait_ge(blocks_done, FULL * TB + tb + 1)
                pe.wait_ge(wl_ready, GU)
                products(banks[tb][:, 0, :], 1, 0, tb).then_inc(gate_done, 1)

            def tile(g, slot, half, first=False):
                pe.wait_ge(il_ready, g + 1)
                wait(pe, y_ready, g - 1)
                dst = banks[slot][:, 0, :]
                for k in range(KT):
                    if first:
                        pe.wait_ge(wdl_ready, half * KT + k + 1)
                    h, l = (v[slot][:, k * P:(k + 1) * P] for v in (ih, il))
                    if k < FULL:
                        pe.matmul(dst, h, wdh[:, k, :], start=(k == 0), stop=False)
                        pe.matmul(dst, h, wdl[:, k, :], start=False, stop=False)
                        i = pe.matmul(dst, l, wdh[:, k, :], start=False, stop=False)
                    else:
                        pe.matmul(dst, h, wdh[:, k, :], start=False, stop=False)
                        i = pe.matmul(dst, h, wdl[:, k, :], start=False, stop=True)
                    i.then_inc(down_step, 1)

            pe.wait_ge(blocks_done, (KT + 1) * TB)
            pe.wait_ge(ih_first, 1)
            dst, h, l = banks[0][:, 0, :], ih[0], il[0]
            for k in range(FULL):
                pe.wait_ge(wdl_ready, k + 1)
                pe.matmul(dst, h[:, k * P:(k + 1) * P], wdh[:, k, :], start=(k == 0), stop=False)
                pe.matmul(dst, h[:, k * P:(k + 1) * P], wdl[:, k, :], start=False, stop=False)
            pe.wait_ge(il_first, 1)
            for k in range(FULL):
                pe.matmul(dst, l[:, k * P:(k + 1) * P], wdh[:, k, :], start=False, stop=False).then_inc(down_step, 1)
            pe.wait_ge(wdl_ready, KT)
            pe.wait_ge(il_ready, 1)
            pe.matmul(dst, h[:, FULL * P:], wdh[:, FULL, :], start=False, stop=False)
            pe.matmul(dst, h[:, FULL * P:], wdl[:, FULL, :], start=False, stop=True).then_inc(down_step, 1)
            for half in range(2):
                g0 = half * TT
                if half:
                    tile(g0, 0, half, True)
                tile(g0 + 1, 1, half)
                with pe.Fori(0, TT // 2 - 1) as q:
                    for s in range(2):
                        tile(q * 2 + (g0 + 2 + s), s, half)


def kernel(x, ctx_4096, L0_ffn_gate_codes, L0_ffn_gate_scales, L0_ffn_up_codes, L0_ffn_up_scales,
           L0_ffn_down_codes, L0_ffn_down_scales):
    import numpy as np
    import concourse.bacc as bacc
    from concourse.bass_utils import run_bass_kernel_spmd as run

    x, ctx = np.ascontiguousarray(x), np.ascontiguousarray(ctx_4096)
    I, H = L0_ffn_gate_codes.shape
    full, half = I // P, I % P

    def turned(codes, scales, a, b):
        c = np.asarray(codes)[a:b].T.reshape(H // P, P, b - a).transpose(1, 0, 2)
        s = np.asarray(scales)[a:b].T.reshape(H // P, 2, b - a).transpose(1, 0, 2)
        return c, s

    gu_c, gu_s = [], []
    for c in range(full):
        for codes, scales in ((L0_ffn_gate_codes, L0_ffn_gate_scales), (L0_ffn_up_codes, L0_ffn_up_scales)):
            a, b = turned(codes, scales, c * P, (c + 1) * P)
            gu_c.append(a.reshape(P, H))
            gu_s.append(b.reshape(2, H))
    g, u = (turned(codes, scales, full * P, I) for codes, scales in
            ((L0_ffn_gate_codes, L0_ffn_gate_scales), (L0_ffn_up_codes, L0_ffn_up_scales)))
    gu_c.append(np.concatenate([g[0], u[0]], axis=2).reshape(P, H))
    gu_s.append(np.concatenate([g[1], u[1]], axis=2).reshape(2, H))

    dc, ds = np.asarray(L0_ffn_down_codes).T, np.asarray(L0_ffn_down_scales).T
    d_c = np.concatenate([dc, dc[full * P:]]).reshape(full + 1, P, H)
    d_s = np.concatenate([ds, ds[2 * full:]]).reshape(full + 1, 2, H)

    arrays = {"x": x, "ctx": ctx, "gu_codes": np.stack(gu_c), "gu_scales": np.stack(gu_s),
              "d_codes": d_c, "d_scales": d_s}
    nc = bacc.Bacc("TRN2", target_bir_lowering=False, num_devices=1, dynamic_dma_scratch_size=1024)
    args, ins = [], {}
    for name, a in arrays.items():
        ins[f"in_{name}"] = np.ascontiguousarray(a)
        args.append(nc.dram_tensor(f"in_{name}", a.shape, mybir.dt.from_np(a.dtype), kind="ExternalInput").ap())
    out = nc.dram_tensor("out_y", x.shape, F32, kind="ExternalOutput").ap()
    xattn_ffn(nc, *args, out)
    r = run(nc, [ins], core_ids=[0])
    return r.results[0]["out_y"]
```

```python
from contextlib import ExitStack

import concourse.bass as bass
from concourse import mybir

F32 = mybir.dt.float32
F32R = mybir.dt.float32r
I32 = mybir.dt.int32
BF16 = mybir.dt.bfloat16
ALU = mybir.AluOpType
ACT = mybir.ActivationFunctionType
AX = mybir.AxisListType

P = 128
HEADS = 8
BLOCK = 64
EPS = 1e-5
WIDE = 512
XS = 4
LR = 4

LINES = [(0.30380716919898987, 1.1266502141952515), (0.1301555633544922, 0.12570476531982422),
         (0.09966795146465302, 0.014562471769750118), (0.09105003625154495, 0.0),
         (0.08134990185499191, -0.0017696022987365723), (0.09180294722318649, -0.02929653413593769),
         (0.12190717458724976, -0.16882604360580444), (0.2770431637763977, -1.2163453102111816)]
CENTRE = 7.0


class Batch:

    def __init__(self, p, j):
        self.n = p * XS + j
        self.xslot, self.xround = j % XS, p + j // XS
        self.slot, self.round = j % 2, p * (XS // 2) + j // 2


class Steps:

    def __init__(self, sem):
        self.sem, self.base, self.local = sem, 0, 0

    def mark(self, ins):
        ins.then_inc(self.sem, 1)
        self.local += 1
        return self.base + self.local

    def enter(self, p, per, first=0):
        start = self.base + self.local - first * per
        self.base, self.local, self.start, self.per = p * per + start, 0, start, per

    def leave(self, end):
        assert self.local == self.per, (self.local, self.per)
        self.base, self.local = self.start + end * self.per, 0


def wait(eng, sem, value):
    if not (isinstance(value, int) and value <= 0):
        eng.wait_ge(sem, value)


def xattn_ffn(nc, x, ctx, gu_codes, gu_scales, d_codes, d_scales, out):
    B, C, N = x.shape
    T = B * C
    GU = gu_codes.shape[0]
    KT = d_codes.shape[0]
    HT = N // P
    TB = T // WIDE
    TT = T // P
    HALF = P // 2
    QT = WIDE // P
    FULL = KT - 1
    ITEM = HT * P
    assert C == P and ITEM == N and GU == 2 * FULL + 1 and N == 2 * WIDE and T == TB * WIDE
    assert B % XS == 0 and B >= 2 * XS and FULL % 2 == 1 and TB == 4
    NI = GU + KT

    x1_dram = nc.dram_tensor("x1_scratch", (B, P, N), F32).ap()
    wd_dram = nc.dram_tensor("wd_scratch", (KT, P, N), F32).ap()
    inter_dram = nc.dram_tensor("inter_scratch", (TT, P, KT, P), F32).ap()

    with ExitStack() as st:
        def sb(name, shape, dt):
            return st.enter_context(nc.sbuf_tensor(name, shape, dt))

        def sem(name):
            return st.enter_context(nc.semaphore(name))

        R1 = sb("R1", [P, 2 * HT * T], F32R)
        R2 = sb("R2", [P, 8 * ITEM], F32R)
        F = sb("F", [P, 15 * N], F32)
        ident = sb("ident", [P, P], F32)
        headmask = sb("headmask", [P, P], F32)
        headsel = sb("headsel", [P, HEADS], F32)
        halfneg = sb("halfneg", [P, 1], F32)
        one = sb("one", [P, 1], F32)
        bn = sb("bn", [P, 2, 6], F32)
        bn2 = sb("bn2", [P, 2, 6], F32)
        mv = sb("mv", [P, 2], F32)
        mv2 = sb("mv2", [P, 2], F32)
        veps = sb("veps", [P, 1], F32)
        veps2 = sb("veps2", [P, 1], F32)
        rstd = sb("rstd", [P, 1], F32)
        rstd2 = sb("rstd2", [P, 1], F32)
        nmr = sb("nmr", [P, 1], F32)
        nmr2 = sb("nmr2", [P, 1], F32)
        nkmax = sb("nkmax", [P, 1], F32)
        ksum = sb("ksum", [P, 1], F32)
        rksum = [sb(f"rksum{s}", [P, 1], F32) for s in range(2)]
        rden = sb("rden", [P, HT * HEADS], F32)
        kvs = sb("kvs", [P, P], F32)

        banks = [st.enter_context(nc.psum_tensor(f"bank{i}", [P, 2, WIDE], F32)) for i in range(4)]

        xh = R1[:, 0:HT * T].rearrange("p (t n) -> p t n", t=HT)
        xl = R1[:, HT * T:2 * HT * T].rearrange("p (t n) -> p t n", t=HT)
        wgu = R2[:, :].rearrange("p (s q g n) -> p s q g n", s=2, q=2, g=2)

        def f(i, n=1):
            return F[:, i * N:(i + n) * N]

        codes = [f(0).bitcast(I32), f(1).bitcast(I32)]
        scales = [f(2), f(3)]
        code7 = [f(4).bitcast(BF16)[:, s * N:(s + 1) * N] for s in range(2)]
        lines = [f(5 + i) for i in range(LR)]
        low, high = f(9), f(10)
        w = [f(11), f(12)]
        silu = [F[:, 13 * N + s * WIDE:13 * N + (s + 1) * WIDE] for s in range(2)]
        inter = [F[:, 14 * N + s * WIDE:14 * N + (s + 1) * WIDE] for s in range(2)]

        xs, cs = [f(13), f(10), f(0), f(12)], [f(14), f(1)]
        x1 = [f(2), f(3)]
        expq = [f(4), f(11)]
        expk, expkT, ctxT, x2, rdenw = [f(5 + i) for i in range(5)]
        pAttn, pX2T, pCtxT = [banks[i][:, :, :].rearrange("p a n -> p (a n)") for i in range(3)]
        pRdenT, pExpkT = pAttn, pCtxT
        pDen = banks[3][:, 0, 0:HT * HEADS]
        pKV = banks[3][:, 1, 0:P]

        HW = KT * WIDE
        IT = KT * P
        wdh = R1[:, 0:HW].rearrange("p (k n) -> p k n", k=KT)
        wdl = R1[:, HW:2 * HW].rearrange("p (k n) -> p k n", k=KT)
        ih = [R2[:, 0:IT], R1[:, 2 * HW:2 * HW + IT]]
        il = [R1[:, 2 * HW + IT:2 * HW + 2 * IT], R1[:, 2 * HW + 2 * IT:2 * HW + 3 * IT]]
        FS = 15
        stage = [F[:, k * WIDE:(k + 1) * WIDE] for k in range(FS)] + \
                [R2[:, IT + (k - FS) * WIDE:IT + (k - FS + 1) * WIDE].bitcast(F32) for k in range(FS, KT)]
        it = [F[:, FS * WIDE + s * IT:FS * WIDE + (s + 1) * IT] for s in range(2)]
        free = FS * WIDE + 2 * IT
        xo = [F[:, free + s * WIDE:free + (s + 1) * WIDE] for s in range(2)]
        yo = [F[:, free + (2 + s) * WIDE:free + (3 + s) * WIDE] for s in range(2)]
        assert 2 * HW + 3 * IT <= 2 * HT * T and IT + (KT - FS) * WIDE <= 8 * ITEM
        assert free >= 13 * N and free + 4 * WIDE <= 15 * N and IT <= 4 * ITEM
        GROUPS = [(0, 4), (4, 8), (8, 12), (12, FS), (FS, KT)]

        consts_ready = sem("consts_ready")
        x_in = [sem(f"x_in{s}") for s in range(XS)]
        ctx_in = [sem(f"ctx_in{s}") for s in range(2)]
        x1_free = [sem(f"x1_free{s}") for s in range(2)]
        veps_ready, rstd_ready, nmr_ready = sem("veps_ready"), sem("rstd_ready"), sem("nmr_ready")
        veps2_ready, rstd2_ready, nmr2_ready = sem("veps2_ready"), sem("rstd2_ready"), sem("nmr2_ready")
        kmax_ready, expq_ready, expk_ready = sem("kmax_ready"), sem("expq_ready"), sem("expk_ready")
        ctx_turned, ctxT_ready = sem("ctx_turned"), sem("ctxT_ready")
        expk_turned, expkT_ready = sem("expk_turned"), sem("expkT_ready")
        den_done, rden_ready, rdenw_ready = sem("den_done"), sem("rden_ready"), sem("rdenw_ready")
        rksum_ready, rden_turned = sem("rksum_ready"), sem("rden_turned")
        kv_done, kvs_ready, softq_ready = sem("kv_done"), sem("kvs_ready"), sem("softq_ready")
        attn_done, x1_ready, x2_ready = sem("attn_done"), sem("x1_ready"), sem("x2_ready")
        x2_turned, xh_ready, xl_ready = sem("x2_turned"), sem("xh_ready"), sem("xl_ready")
        codes_in = [sem(f"codes_in{s}") for s in range(2)]
        scales_in = [sem(f"scales_in{s}") for s in range(2)]
        code7_ready, line_ready, lines_merged = sem("code7_ready"), sem("line_ready"), sem("lines_merged")
        w_ready, wh_ready, wl_ready = sem("w_ready"), sem("wh_ready"), sem("wl_ready")
        wd_stored = [sem(f"wd_stored{s}") for s in range(2)]
        gate_done, up_done, silu_ready = sem("gate_done"), sem("up_done"), sem("silu_ready")
        blocks_done = sem("blocks_done")
        up_copied = sem("up_copied")
        inter_stored = [sem(f"inter_stored{s}") for s in range(2)]
        stage_in = [sem(f"stage_in{g}") for g in range(len(GROUPS))]
        wdh_ready, wdl_ready = sem("wdh_ready"), sem("wdl_ready")
        inter_in = [sem(f"inter_in{s}") for s in range(2)]
        last_in = [sem(f"last_in{s}") for s in range(2)]
        x1_in = [sem(f"x1_in{s}") for s in range(2)]
        ih_ready, il_ready = sem("ih_ready"), sem("il_ready")
        ih_first, il_first = sem("ih_first"), sem("il_first")
        down_step, y_ready = sem("down_step"), sem("y_ready")
        y_stored = [sem(f"y_stored{s}") for s in range(2)]
        dve_step = sem("dve_step")
        pool_step = sem("pool_step")

        NCONST = 3
        LOOPS = B // XS - 1
        PAIRS = FULL // 2
        TILES = 2 * TT

        def batch(p, k, d):
            if isinstance(p, int) and not 0 <= p * XS + k - d < B:
                return None
            return Batch(p, k - d)

        def mixer(engine, turn, stages, before=None, after=None):
            for k in range(XS):
                turn(0, k)
            with engine.Fori(0, LOOPS) as p:
                if before:
                    before(p)
                for k in range(XS, 2 * XS):
                    turn(p, k)
            if after:
                after()
            for k in range(XS, XS + stages - 1):
                turn(LOOPS, k)

        def tokens_of(v, t):
            return v[:, :, t.n * P:(t.n + 1) * P] if isinstance(t.n, int) else v[:, :, bass.ds(t.n * P, P)]

        block = st.enter_context(nc.Block())

        @block.sync
        def _(sp):
            def load_codes(n, slot, src):
                sp.dma_start(codes[slot], src).then_inc(codes_in[slot], 16)

            def load_scales(n, slot, src):
                sp.dma_start(scales[slot], src.unsqueeze(1).to_broadcast([2, BLOCK, ITEM])).then_inc(scales_in[slot], 16)

            def at(a, i):
                return a[i] if isinstance(i, int) else a[bass.ds(i, 1)].rearrange("o p n -> (o p) n")

            def load_item(n, slot, cod, scl, i):
                wait(sp, code7_ready, n - 1)
                load_codes(n, slot, at(cod, i))
                wait(sp, w_ready, n - 1)
                load_scales(n, slot, at(scl, i))

            def load_x(b):
                sp.dma_start(xs[b.xslot], at(x, b.n)).then_inc(x_in[b.xslot], 16)

            def load_ctx(b):
                sp.dma_start(cs[b.slot], at(ctx, b.n)).then_inc(ctx_in[b.slot], 16)

            load_item(0, 0, gu_codes, gu_scales, 0)
            load_item(1, 1, gu_codes, gu_scales, 1)

            def mixer_turn(p, k):
                b, old = batch(p, k, 0), batch(p, k, XS)
                if old:
                    sp.wait_ge(x1_ready, old.n + 1)
                if b and batch(p, k, 2):
                    load_x(b)
                    sp.wait_ge(ctx_turned, b.n - 1)
                    sp.wait_ge(expk_ready, b.n - 1)
                    load_ctx(b)
                if old:
                    sp.dma_start(at(x1_dram, old.n), x1[old.slot]).then_inc(x1_free[old.slot], 16)

            load_x(Batch(0, 0))
            load_ctx(Batch(0, 0))
            sp.wait_ge(wl_ready, 2)
            load_x(Batch(0, 1))
            load_ctx(Batch(0, 1))
            mixer(sp, mixer_turn, XS + 1)

            sp.wait_ge(xl_ready, B)
            for s in range(2):
                sp.wait_ge(x1_free[s], 16 + B // 2 * 16)
            load_item(2, 0, d_codes, d_scales, 0)
            load_item(3, 1, gu_codes, gu_scales, 2)

            def store_block(c, tb, rows=None):
                s = tb % 2
                sp.wait_ge(blocks_done, c * TB + tb + 1 + TB)
                if rows is None:
                    dst = inter_dram[tb * QT:(tb + 1) * QT, :, bass.ds(c, 1), :].rearrange("q p o n -> p (q o) n")
                    sp.dma_start(dst, inter[s].rearrange("p (q n) -> p q n", q=QT)).then_inc(inter_stored[s], 16)
                    return
                for a in range(2):
                    dst = inter_dram[tb * QT:(tb + 1) * QT, a * HALF:(a + 1) * HALF, c, :].rearrange("q p n -> p q n")
                    sp.dma_start(dst, inter[s][0:HALF, :].rearrange("p (q n) -> p q n", q=QT)).then_inc(inter_stored[s], 16)

            def store_wd(c, par):
                sp.wait_ge(w_ready, c * 3 + 3)
                sp.dma_start(at(wd_dram, c), w[par]).then_inc(wd_stored[par], 16)

            with sp.Fori(0, PAIRS) as p:
                for j in range(2):
                    c = p * 2 + j
                    n = p * 6 + 2 + 3 * j
                    load_item(n + 2, j, gu_codes, gu_scales, c * 2 + 3)
                    store_wd(c, j)
                    store_block(c, 0)
                    load_item(n + 3, 1 - j, d_codes, d_scales, c + 1)
                    store_block(c, 1)
                    load_item(n + 4, j, gu_codes, gu_scales, c * 2 + 4)
                    store_block(c, 2)
                    store_block(c, 3)
            c = FULL - 1
            load_item(NI - 1, 0, d_codes, d_scales, KT - 1)
            store_wd(c, c % 2)
            store_block(c, 0)
            store_block(c, 1)
            sp.wait_ge(w_ready, NI)
            sp.dma_start(wd_dram[KT - 1], w[0]).then_inc(wd_stored[0], 16)
            store_block(c, 2)
            store_block(c, 3)
            sp.wait_ge(wd_stored[0], 16 * (FULL // 2 + 2))
            sp.wait_ge(wd_stored[1], 16 * (FULL // 2))

            def load_stage(half, g):
                a, b = GROUPS[g]
                src = wd_dram[a:b, :, half * WIDE:(half + 1) * WIDE].rearrange("k p n -> p k n")
                if a < FS:
                    dst = F[:, a * WIDE:b * WIDE].rearrange("p (k n) -> p k n", n=WIDE)
                else:
                    dst = R2[:, IT:IT + (b - a) * WIDE].bitcast(F32).rearrange("p (k n) -> p k n", n=WIDE)
                sp.dma_start(dst, src).then_inc(stage_in[g], 16)

            def load_tile(t, slot, half, cols=(0, KT)):
                g = t + half * TT
                wait(sp, il_ready, g - 1)
                a, b = cols
                dst = it[slot][:, a * P:b * P].rearrange("p (k n) -> p k n", n=P)
                src = inter_dram[t] if isinstance(t, int) else \
                    inter_dram[bass.ds(t, 1)].rearrange("o p k n -> (o p) k n")
                sp.dma_start(dst, src[:, a:b, :]).then_inc(inter_in[slot], 16)

            for s in range(2):
                sp.wait_ge(inter_stored[s], 16 * 2 * FULL)
            load_tile(0, 0, 0, (0, FULL))
            for g in range(len(GROUPS) - 1):
                load_stage(0, g)
            load_tile(1, 1, 0, (0, FULL))
            for tb in range(TB):
                store_block(FULL, tb, HALF)
            sp.wait_ge(gate_done, TB * KT)
            load_stage(0, len(GROUPS) - 1)
            for s in range(2):
                sp.wait_ge(inter_stored[s], 16 * (2 * FULL + 4))
            for t in range(2):
                sp.dma_start(it[t][:, FULL * P:], inter_dram[t, :, FULL, :]).then_inc(last_in[t], 16)

            def load_x1(t, slot, half):
                sp.dma_start(xo[slot], at(x1_dram, t)[:, half * WIDE:(half + 1) * WIDE]).then_inc(x1_in[slot], 16)

            def store_y(t, slot, half):
                sp.wait_ge(y_ready, t + half * TT + 1)
                sp.dma_start(at(out, t)[:, half * WIDE:(half + 1) * WIDE], yo[slot]).then_inc(y_stored[slot], 16)

            for half in range(2):
                for t in range(2):
                    if half:
                        load_tile(t, t, half)
                    if half:
                        store_y(TT - 2 + t, t, half - 1)
                    load_x1(t, t, half)
                if half == 0:
                    for g in range(len(GROUPS)):
                        sp.wait_ge(wdl_ready, GROUPS[g][1])
                        load_stage(1, g)
                with sp.Fori(0, TT // 2 - 1) as q:
                    for s in range(2):
                        t = q * 2 + 2 + s
                        load_tile(t, s, half)
                        store_y(t - 2, s, half)
                        load_x1(t, s, half)
            for s in range(2):
                store_y(TT - 2 + s, s, 1)
            for s in range(2):
                sp.wait_ge(y_stored[s], 16 * TT)

        @block.gpsimd
        def _(pool):
            own = Steps(pool_step)
            m = [own.mark(nc.gpsimd.memset(a, v)) for a, v in
                 ((ident[:, :], 0.0), (headmask[:, :], 1.0), (headsel[:, :], 1.0), (halfneg[:, :], -0.5), (one[:, :], 1.0))]
            pool.wait_ge(pool_step, m[-1])
            nc.gpsimd.affine_select(out=ident[:, :], in_=ident[:, :], compare_op=ALU.not_equal, fill=1.0, base=0,
                                    pattern=[[-1, P]], channel_multiplier=1).then_inc(consts_ready, 1)
            D = P // HEADS
            for a, cols in ((headmask[:, :].rearrange("p (h d) -> p h d", h=HEADS), D), (headsel[:, :].unsqueeze(2), 1)):
                k = own.mark(nc.gpsimd.affine_select(out=a, in_=a, compare_op=ALU.is_ge, fill=0.0, base=0,
                                                     pattern=[[-D, HEADS], [0, cols]], channel_multiplier=1))
                pool.wait_ge(pool_step, k)
                nc.gpsimd.affine_select(out=a, in_=a, compare_op=ALU.is_ge, fill=0.0, base=D - 1,
                                        pattern=[[D, HEADS], [0, cols]], channel_multiplier=-1).then_inc(consts_ready, 1)

            def power(src_ready, n, dst, src, ready):
                pool.wait_ge(src_ready, n + 1)
                nc.gpsimd.tensor_tensor(dst, src, halfneg[:, :], ALU.pow).then_inc(ready, 1)

            def mixer_turn(p, k):
                a, b, c = batch(p, k, 0), batch(p, k, 3), batch(p, k, 1)
                if a:
                    wait(pool, expq_ready, a.n)
                    power(veps_ready, a.n, rstd[:, :], veps[:, :], rstd_ready)
                if b:
                    wait(pool, x2_ready, b.n)
                    power(veps2_ready, b.n, rstd2[:, :], veps2[:, :], rstd2_ready)
                if c:
                    pool.wait_ge(rden_ready, c.n + 1)
                    wait(pool, rden_turned, c.n)
                    nc.gpsimd.tensor_tensor(rdenw.rearrange("p (t d) -> p t d", d=D),
                                            rden[:, :].unsqueeze(2).to_broadcast([P, HT * HEADS, D]),
                                            one[:, :].unsqueeze(2).to_broadcast([P, HT * HEADS, D]),
                                            ALU.mult).then_inc(rdenw_ready, 1)

            mixer(pool, mixer_turn, 4)

        def lines_of(act, n, s, middle=None):
            act.wait_ge(code7_ready, n + 1)
            for q in range(8):
                if q < LR:
                    wait(act, lines_merged, (n - 1) * 6 + [4, 4, 5, 6][q])
                else:
                    act.wait_ge(lines_merged, n * 6 + [1, 1, 2, 3][q - LR])
                slope, offset = LINES[q]
                nc.scalar.activation(lines[q % LR], code7[s], ACT.Copy, bias=offset, scale=slope).then_inc(line_ready, 1)
                if q == LR - 1 and middle:
                    middle()

        @block.scalar
        def _(act):
            def hi_of(n, s, c, g, par):
                act.wait_ge(w_ready, n + 1)
                wait(act, up_done, (c - 1) * TB)
                nc.scalar.activation(wgu[:, par, 0, g], w[s], ACT.Copy).then_inc(wh_ready, 1)

            def mixer_turn(p, k):
                a, b, c = batch(p, k, 0), batch(p, k, 3), batch(p, k, 2)
                if a:
                    act.wait_ge(nmr_ready, a.n + 1)
                    wait(act, attn_done, a.n - 1)
                    nc.scalar.activation(expq[a.slot], xs[a.xslot], ACT.Exp, bias=nmr[:, :], scale=rstd[:, :]).then_inc(expq_ready, 1)
                    act.wait_ge(kmax_ready, a.n + 1)
                    wait(act, expk_turned, a.n)
                    wait(act, rksum_ready, a.n)
                    nc.scalar.activation(expk, cs[a.slot], ACT.Exp, bias=nkmax[:, :], accum_out=ksum[:, :]).then_inc(expk_ready, 1)
                if b:
                    act.wait_ge(x2_turned, b.n + 1)
                    nc.scalar.copy(tokens_of(xh, b), pX2T.rearrange("p (t n) -> p t n", t=HT)).then_inc(xh_ready, 1)
                if a:
                    act.wait_ge(ctx_turned, a.n + 1)
                    wait(act, kv_done, a.n)
                    nc.scalar.copy(ctxT, pCtxT).then_inc(ctxT_ready, 1)
                    act.wait_ge(expk_turned, a.n + 1)
                    nc.scalar.copy(expkT, pExpkT).then_inc(expkT_ready, 1)
                if c:
                    act.wait_ge(nmr2_ready, c.n + 1)
                    nc.scalar.activation(x2, x1[c.slot], ACT.Identity, bias=nmr2[:, :], scale=rstd2[:, :]).then_inc(x2_ready, 1)

            lines_of(act, 0, 0)
            hi_of(0, 0, 0, 0, 0)
            lines_of(act, 1, 1)
            hi_of(1, 1, 0, 1, 0)
            mixer(act, mixer_turn, 4)

            def silu_of(c, tb):
                act.wait_ge(gate_done, c * TB + tb + 1)
                act.wait_ge(blocks_done, c * TB + tb - 1 + TB)
                nc.scalar.activation(silu[tb % 2], banks[tb][:, 0, :], ACT.Silu).then_inc(silu_ready, 1)

            def chunk_pair(p):
                for j in range(2):
                    c = p * 2 + j
                    n = p * 6 + 2 + 3 * j
                    lines_of(act, n, j)
                    silu_of(c, 0)
                    lines_of(act, n + 1, 1 - j)
                    silu_of(c, 1)
                    lines_of(act, n + 2, j, lambda: hi_of(n + 1, 1 - j, c + 1, 0, 1 - j))
                    hi_of(n + 2, j, c + 1, 1, 1 - j)
                    silu_of(c, 2)
                    silu_of(c, 3)

            chunk_pair(0)
            with act.Fori(1, PAIRS) as p:
                chunk_pair(p)
            c = FULL - 1
            lines_of(act, NI - 3, 0)
            silu_of(c, 0)
            lines_of(act, NI - 2, 1)
            hi_of(NI - 2, 1, FULL, 0, 1)
            silu_of(c, 1)
            lines_of(act, NI - 1, 0)
            silu_of(c, 2)
            silu_of(c, 3)
            for tb in range(TB):
                s = tb % 2
                act.wait_ge(gate_done, FULL * TB + tb + 1)
                act.wait_ge(blocks_done, FULL * TB + tb - 1 + TB)
                nc.scalar.activation(silu[s][0:HALF, :], banks[tb][0:HALF, 0, :], ACT.Silu).then_inc(silu_ready, 1)
                act.wait_ge(inter_stored[s], 16 * (2 * FULL + 2 * (tb // 2)))
                nc.scalar.copy(inter[s][0:HALF, :], banks[tb][HALF:P, 0, :]).then_inc(up_copied, 1)

            def split_weights(half):
                for g, (a, b) in enumerate(GROUPS):
                    act.wait_ge(stage_in[g], 16 * (half + 1))
                    for k in range(a, b):
                        if half:
                            act.wait_ge(down_step, KT * (TT - 1) + k + 1)
                        nc.scalar.copy(wdh[:, k, :], stage[k]).then_inc(wdh_ready, 1)

            def split_tile(g, slot, uses):
                act.wait_ge(inter_in[slot], uses)
                wait(act, down_step, (g - 1) * KT)
                nc.scalar.copy(ih[slot], it[slot]).then_inc(ih_ready, 1)

            act.wait_ge(inter_in[0], 16)
            act.wait_ge(up_done, FULL * TB)
            nc.scalar.copy(ih[0][:, 0:FULL * P], it[0][:, 0:FULL * P]).then_inc(ih_first, 1)
            act.wait_ge(gate_done, TB * KT)
            split_weights(0)
            act.wait_ge(last_in[0], 16)
            nc.scalar.copy(ih[0][:, FULL * P:], it[0][:, FULL * P:]).then_inc(ih_ready, 1)
            act.wait_ge(last_in[1], 16)
            split_tile(1, 1, 16)
            for half in range(2):
                g0, u0 = half * TT, 16 * half * TT // 2
                if half:
                    split_tile(g0, 0, u0 + 16)
                    split_weights(half)
                    split_tile(g0 + 1, 1, u0 + 16)
                with act.Fori(0, TT // 2 - 1) as q:
                    for s in range(2):
                        split_tile(q * 2 + (g0 + 2 + s), s, q * 16 + (u0 + 32))

        @block.vector
        def _(dve):
            own = Steps(dve_step)

            def after(token):
                dve.wait_ge(dve_step, token)

            for i in range(TB):
                nc.vector.memset(bn[:, 0, i:i + 1], 0.0).then_inc(blocks_done, 1)
            for s in range(2):
                nc.vector.memset(bn[:, 1, s:s + 1], 0.0).then_inc(x1_free[s], 16)

            def centre(n, s):
                dve.wait_ge(codes_in[s], centre_round(n))
                nc.vector.tensor_scalar(code7[s], codes[s], CENTRE, None, ALU.subtract).then_inc(code7_ready, 1)

            def centre_round(n):
                return 16 * (n // 2 + 1)

            def merge(n, s, round_, middle=None, w_free=None):
                at = lambda q: lines[q % LR]
                vt = nc.vector
                dve.wait_ge(line_ready, n * 8 + 2)
                vt.scalar_tensor_tensor(low, at(0), 0.0, at(1), ALU.min, ALU.min).then_inc(lines_merged, 1)
                for q in (2, 3):
                    dve.wait_ge(line_ready, n * 8 + q + 1)
                    dve.wait_ge(lines_merged, n * 6 + q - 1)
                    vt.tensor_tensor(low, low, at(q), ALU.min).then_inc(lines_merged, 1)
                if middle:
                    middle()
                dve.wait_ge(line_ready, n * 8 + 6)
                vt.tensor_tensor(high, at(4), at(5), ALU.max).then_inc(lines_merged, 1)
                for q in (6, 7):
                    dve.wait_ge(line_ready, n * 8 + q + 1)
                    dve.wait_ge(lines_merged, n * 6 + q - 2)
                    vt.tensor_tensor(high, high, at(q), ALU.max).then_inc(lines_merged, 1)
                if w_free:
                    dve.wait_ge(*w_free)
                dve.wait_ge(lines_merged, n * 6 + 6)
                after(own.mark(vt.scalar_tensor_tensor(w[s], high, 0.0, low, ALU.max, ALU.add)))
                dve.wait_ge(scales_in[s], round_)
                vt.tensor_tensor(w[s], w[s], scales[s], ALU.mult).then_inc(w_ready, 1)

            def lo_of(m, s, g, par):
                dve.wait_ge(wh_ready, m + 1)
                nc.vector.tensor_tensor(wgu[:, par, 1, g], w[s], wgu[:, par, 0, g].bitcast(F32), ALU.subtract).then_inc(wl_ready, 1)

            for n in range(2):
                centre(n, n)
                merge(n, n, 16)
                dve.wait_ge(w_ready, n + 1)
                lo_of(n, n, n, 0)

            def stats(src, bn_, mv_, veps_, ready):
                for i in range(2):
                    nc.vector.bn_stats(bn_[:, i, :], src[:, i * WIDE:(i + 1) * WIDE])
                dve.drain()
                after(own.mark(nc.vector.bn_aggr(mv_[:, :], bn_[:, :, :].rearrange("p a n -> p (a n)"))))
                nc.vector.tensor_scalar(veps_[:, :], mv_[:, 1:2], EPS, None, ALU.add).then_inc(ready, 1)

            def mixer_turn(p, k):
                a, b, c, d, e = [batch(p, k, i) for i in range(5)]
                if a:
                    dve.wait_ge(x_in[a.xslot], (a.xround + 1) * 16)
                    stats(xs[a.xslot], bn, mv, veps, veps_ready)
                if d:
                    dve.wait_ge(attn_done, d.n + 1)
                    dve.wait_ge(x1_free[d.slot], (d.round + 1) * 16)
                    nc.vector.tensor_tensor(x1[d.slot], xs[d.xslot], pAttn, ALU.add).then_inc(x1_ready, 1)
                    dve.wait_ge(x1_ready, d.n + 1)
                    stats(x1[d.slot], bn2, mv2, veps2, veps2_ready)
                if a:
                    dve.wait_ge(rstd_ready, a.n + 1)
                    nc.vector.scalar_tensor_tensor(nmr[:, :], mv[:, 0:1], -1.0, rstd[:, :], ALU.mult, ALU.mult).then_inc(nmr_ready, 1)
                if c:
                    dve.wait_ge(kv_done, c.n + 1)
                    dve.wait_ge(rksum_ready, c.n + 1)
                    nc.vector.scalar_tensor_tensor(kvs[:, :], pKV, rksum[c.slot][:, :], headmask[:, :], ALU.mult, ALU.mult).then_inc(kvs_ready, 1)
                if b:
                    dve.wait_ge(expk_ready, b.n + 1)
                    nc.vector.reciprocal(rksum[b.slot][:, :], ksum[:, :]).then_inc(rksum_ready, 1)
                if c:
                    dve.wait_ge(rden_turned, c.n + 1)
                    nc.vector.tensor_tensor(expq[c.slot], expq[c.slot], pRdenT, ALU.mult).then_inc(softq_ready, 1)
                if a:
                    dve.wait_ge(ctx_in[a.slot], (a.round + 1) * 16)
                    nc.vector.tensor_reduce(nkmax[:, :], cs[a.slot], AX.X, ALU.max, negate=True).then_inc(kmax_ready, 1)
                if d:
                    dve.wait_ge(rstd2_ready, d.n + 1)
                    nc.vector.scalar_tensor_tensor(nmr2[:, :], mv2[:, 0:1], -1.0, rstd2[:, :], ALU.mult, ALU.mult).then_inc(nmr2_ready, 1)
                if e:
                    dve.wait_ge(xh_ready, e.n + 1)
                    h, l = (tokens_of(v, e) for v in (xh, xl))
                    nc.vector.tensor_tensor(l, pX2T.rearrange("p (t n) -> p t n", t=HT), h.bitcast(F32), ALU.subtract).then_inc(xl_ready, 1)
                if b:
                    dve.wait_ge(den_done, b.n + 1)
                    nc.vector.reciprocal(rden[:, :], pDen).then_inc(rden_ready, 1)

            dve.wait_ge(consts_ready, NCONST)
            mixer(dve, mixer_turn, 5, lambda p: own.enter(p, XS * 2), lambda: own.leave(LOOPS))

            def block_out(c, tb):
                dve.wait_ge(silu_ready, c * TB + tb + 1)
                dve.wait_ge(up_done, c * TB + tb + 1)
                wait(dve, inter_stored[tb % 2], c * 32 + 16 * (tb // 2))
                nc.vector.tensor_tensor(inter[tb % 2], silu[tb % 2], banks[tb][:, 1, :], ALU.mult).then_inc(blocks_done, 1)

            centre(2, 0)
            def chunk_pair(p):
                for j in range(2):
                    c = p * 2 + j
                    n = p * 6 + 2 + 3 * j

                    def centre_in(k, s):
                        dve.wait_ge(codes_in[s], p * 48 + 16 * (k // 2 + 1))
                        nc.vector.tensor_scalar(code7[s], codes[s], CENTRE, None, ALU.subtract).then_inc(code7_ready, 1)

                    def round_in(k):
                        return p * 48 + 16 * (k // 2 + 1)

                    k = 2 + 3 * j
                    merge(n, j, round_in(k), lambda: centre_in(k + 1, 1 - j))
                    block_out(c, 0)
                    merge(n + 1, 1 - j, round_in(k + 1), lambda: centre_in(k + 2, j))
                    block_out(c, 1)

                    def middle():
                        dve.wait_ge(w_ready, n + 2)
                        lo_of(c * 2 + 2, 1 - j, 0, 1 - j)
                        centre_in(k + 3, 1 - j)
                    merge(n + 2, j, round_in(k + 2), middle, (wd_stored[j], p * 16 + 16))
                    dve.wait_ge(w_ready, n + 3)
                    lo_of(c * 2 + 3, j, 1, 1 - j)
                    block_out(c, 2)
                    block_out(c, 3)

            chunk_pair(0)
            with dve.Fori(1, PAIRS) as p:
                own.enter(p, 6, first=1)
                chunk_pair(p)
            own.leave(PAIRS)

            c = FULL - 1

            def centre_last(n, s):
                dve.wait_ge(codes_in[s], 16 * (n // 2 + 1))
                nc.vector.tensor_scalar(code7[s], codes[s], CENTRE, None, ALU.subtract).then_inc(code7_ready, 1)

            merge(NI - 3, 0, 16 * ((NI - 3) // 2 + 1), lambda: centre_last(NI - 2, 1))
            block_out(c, 0)
            merge(NI - 2, 1, 16 * ((NI - 2) // 2 + 1), lambda: centre_last(NI - 1, 0))
            dve.wait_ge(w_ready, NI - 1)
            lo_of(2 * FULL, 1, 0, 1)
            block_out(c, 1)
            merge(NI - 1, 0, 16 * ((NI - 1) // 2 + 1), None, (wd_stored[0], 16 * (FULL // 2 + 1)))
            block_out(c, 2)
            block_out(c, 3)
            for tb in range(TB):
                s = tb % 2
                dve.wait_ge(silu_ready, FULL * TB + tb + 1)
                dve.wait_ge(up_copied, tb + 1)
                nc.vector.tensor_tensor(inter[s][0:HALF, :], inter[s][0:HALF, :], silu[s][0:HALF, :], ALU.mult).then_inc(blocks_done, 1)

            def split_weights(half):
                for k in range(KT):
                    dve.wait_ge(wdh_ready, half * KT + k + 1)
                    nc.vector.tensor_tensor(wdl[:, k, :], stage[k], wdh[:, k, :].bitcast(F32), ALU.subtract).then_inc(wdl_ready, 1)

            def lo_full(slot):
                h = ih[slot].bitcast(F32)
                return nc.vector.tensor_tensor(il[slot][:, 0:FULL * P], it[slot][:, 0:FULL * P], h[:, 0:FULL * P], ALU.subtract)

            def lo_last(slot):
                h = ih[slot].bitcast(F32)
                nc.vector.tensor_tensor(ih[slot][HALF:P, FULL * P:], it[slot][HALF:P, FULL * P:], h[HALF:P, FULL * P:],
                                        ALU.subtract).then_inc(il_ready, 1)

            def split_tile(g, slot):
                dve.wait_ge(ih_ready, g + 1)
                lo_full(slot)
                lo_last(slot)

            def tile_out(g, slot, uses):
                dve.wait_ge(down_step, (g + 1) * KT)
                dve.wait_ge(x1_in[slot], uses)
                wait(dve, y_stored[slot], uses - 16)
                nc.vector.tensor_tensor(yo[slot], xo[slot], banks[slot][:, 0, :], ALU.add).then_inc(y_ready, 1)

            for s in range(2):
                dve.wait_ge(inter_stored[s], 16 * (2 * FULL + 4))
            for half in range(2):
                g0 = half * TT
                if half:
                    split_tile(g0, 0)
                    split_weights(half)
                    tile_out(g0 - 1, 1, 16 * (TT // 2))
                else:
                    split_weights(half)
                    dve.wait_ge(ih_first, 1)
                    lo_full(0).then_inc(il_first, 1)
                    dve.wait_ge(ih_ready, 1)
                    lo_last(0)
                split_tile(g0 + 1, 1)
                tile_out(g0, 0, 16 * (half * TT // 2 + 1))
                split_tile(g0 + 2, 0)
                tile_out(g0 + 1, 1, 16 * (half * TT // 2 + 1))
                with dve.Fori(0, TT // 2 - 2) as q:
                    for s in range(2):
                        g = q * 2 + (g0 + 3 + s)
                        split_tile(g, 1 - s)
                        tile_out(g - 1, s, q * 16 + 16 * (half * TT // 2 + 2))
                split_tile(g0 + TT - 1, 1)
                tile_out(g0 + TT - 2, 0, 16 * (half + 1) * TT // 2)
            tile_out(TILES - 1, 1, 16 * TT)

        @block.tensor
        def _(pe):
            def turn_tiles(dst, src):
                for t in range(HT):
                    i = pe.transpose(dst[:, t * P:(t + 1) * P], src[:, t * P:(t + 1) * P], ident[:, :])
                return i

            def mixer_turn(p, k):
                a, b, c = [batch(p, k, i) for i in range(3)]
                if a:
                    pe.wait_ge(ctx_in[a.slot], (a.round + 1) * 16)
                    wait(pe, expkT_ready, a.n)
                    turn_tiles(pCtxT, cs[a.slot]).then_inc(ctx_turned, 1)
                if b:
                    pe.wait_ge(rdenw_ready, b.n + 1)
                    wait(pe, x1_ready, b.n)
                    turn_tiles(pRdenT, rdenw).then_inc(rden_turned, 1)
                if a:
                    pe.wait_ge(expq_ready, a.n + 1)
                    wait(pe, rden_ready, a.n)
                    for t in range(HT):
                        i = pe.matmul(pDen[:, t * HEADS:(t + 1) * HEADS], expq[a.slot][:, t * P:(t + 1) * P], headsel[:, :],
                                      start=True, stop=True)
                    i.then_inc(den_done, 1)
                    pe.wait_ge(expk_ready, a.n + 1)
                    pe.wait_ge(ctxT_ready, a.n + 1)
                    turn_tiles(pExpkT, expk).then_inc(expk_turned, 1)
                if b:
                    pe.wait_ge(kvs_ready, b.n + 1)
                    pe.wait_ge(softq_ready, b.n + 1)
                    for h in range(2):
                        i = pe.matmul(pAttn[:, h * WIDE:(h + 1) * WIDE], kvs[:, :], expq[b.slot][:, h * WIDE:(h + 1) * WIDE],
                                      start=True, stop=True)
                    i.then_inc(attn_done, 1)
                if a:
                    pe.wait_ge(expkT_ready, a.n + 1)
                    wait(pe, kvs_ready, a.n)
                    for t in range(HT):
                        i = pe.matmul(pKV, expkT[:, t * P:(t + 1) * P], ctxT[:, t * P:(t + 1) * P],
                                      start=(t == 0), stop=(t == HT - 1))
                    i.then_inc(kv_done, 1)
                if c:
                    pe.wait_ge(x2_ready, c.n + 1)
                    wait(pe, xl_ready, c.n)
                    turn_tiles(pX2T, x2).then_inc(x2_turned, 1)

            pe.wait_ge(consts_ready, NCONST)
            mixer(pe, mixer_turn, 3)

            def products(dst, par, g, tb):
                for t in range(HT):
                    hi, lo = (wgu[:, par, q, g, t * P:(t + 1) * P] for q in range(2))
                    cols = slice(tb * WIDE, (tb + 1) * WIDE)
                    pe.matmul(dst, hi, xh[:, t, cols], start=(t == 0), stop=False)
                    pe.matmul(dst, hi, xl[:, t, cols], start=False, stop=False)
                    i = pe.matmul(dst, lo, xh[:, t, cols], start=False, stop=(t == HT - 1))
                return i

            def chunk(c, par):
                for tb in range(TB):
                    pe.wait_ge(blocks_done, c * TB + tb + 1)
                    if tb == 0:
                        pe.wait_ge(wl_ready, c * 2 + 1)
                    products(banks[tb][:, 0, :], par, 0, tb).then_inc(gate_done, 1)
                    if tb == 0:
                        pe.wait_ge(wl_ready, c * 2 + 2)
                    products(banks[tb][:, 1, :], par, 1, tb).then_inc(up_done, 1)

            pe.wait_ge(xl_ready, B)
            with pe.Fori(0, PAIRS) as p:
                for j in range(2):
                    chunk(p * 2 + j, j)
            chunk(FULL - 1, 0)
            for tb in range(TB):
                pe.wait_ge(blocks_done, FULL * TB + tb + 1)
                pe.wait_ge(wl_ready, GU)
                products(banks[tb][:, 0, :], 1, 0, tb).then_inc(gate_done, 1)

            def tile(g, slot, half, first=False):
                pe.wait_ge(il_ready, g + 1)
                wait(pe, y_ready, g - 1)
                dst = banks[slot][:, 0, :]
                for k in range(KT):
                    if first:
                        pe.wait_ge(wdl_ready, half * KT + k + 1)
                    h, l = (v[slot][:, k * P:(k + 1) * P] for v in (ih, il))
                    if k < FULL:
                        pe.matmul(dst, h, wdh[:, k, :], start=(k == 0), stop=False)
                        pe.matmul(dst, h, wdl[:, k, :], start=False, stop=False)
                        i = pe.matmul(dst, l, wdh[:, k, :], start=False, stop=False)
                    else:
                        pe.matmul(dst, h, wdh[:, k, :], start=False, stop=False)
                        i = pe.matmul(dst, h, wdl[:, k, :], start=False, stop=True)
                    i.then_inc(down_step, 1)

            pe.wait_ge(blocks_done, (KT + 1) * TB)
            pe.wait_ge(ih_first, 1)
            dst, h, l = banks[0][:, 0, :], ih[0], il[0]
            for k in range(FULL):
                pe.wait_ge(wdl_ready, k + 1)
                pe.matmul(dst, h[:, k * P:(k + 1) * P], wdh[:, k, :], start=(k == 0), stop=False)
                pe.matmul(dst, h[:, k * P:(k + 1) * P], wdl[:, k, :], start=False, stop=False)
            pe.wait_ge(il_first, 1)
            for k in range(FULL):
                pe.matmul(dst, l[:, k * P:(k + 1) * P], wdh[:, k, :], start=False, stop=False).then_inc(down_step, 1)
            pe.wait_ge(wdl_ready, KT)
            pe.wait_ge(il_ready, 1)
            pe.matmul(dst, h[:, FULL * P:], wdh[:, FULL, :], start=False, stop=False)
            pe.matmul(dst, h[:, FULL * P:], wdl[:, FULL, :], start=False, stop=True).then_inc(down_step, 1)
            for half in range(2):
                g0 = half * TT
                if half:
                    tile(g0, 0, half, True)
                tile(g0 + 1, 1, half)
                with pe.Fori(0, TT // 2 - 1) as q:
                    for s in range(2):
                        tile(q * 2 + (g0 + 2 + s), s, half)


def kernel(x, ctx_4096, L0_ffn_gate_codes, L0_ffn_gate_scales, L0_ffn_up_codes, L0_ffn_up_scales,
           L0_ffn_down_codes, L0_ffn_down_scales):
    import numpy as np
    import concourse.bacc as bacc
    from concourse.bass_utils import run_bass_kernel_spmd as run

    x, ctx = np.ascontiguousarray(x), np.ascontiguousarray(ctx_4096)
    I, H = L0_ffn_gate_codes.shape
    full, half = I // P, I % P

    def turned(codes, scales, a, b):
        c = np.asarray(codes)[a:b].T.reshape(H // P, P, b - a).transpose(1, 0, 2)
        s = np.asarray(scales)[a:b].T.reshape(H // P, 2, b - a).transpose(1, 0, 2)
        return c, s

    gu_c, gu_s = [], []
    for c in range(full):
        for codes, scales in ((L0_ffn_gate_codes, L0_ffn_gate_scales), (L0_ffn_up_codes, L0_ffn_up_scales)):
            a, b = turned(codes, scales, c * P, (c + 1) * P)
            gu_c.append(a.reshape(P, H))
            gu_s.append(b.reshape(2, H))
    g, u = (turned(codes, scales, full * P, I) for codes, scales in
            ((L0_ffn_gate_codes, L0_ffn_gate_scales), (L0_ffn_up_codes, L0_ffn_up_scales)))
    gu_c.append(np.concatenate([g[0], u[0]], axis=2).reshape(P, H))
    gu_s.append(np.concatenate([g[1], u[1]], axis=2).reshape(2, H))

    dc, ds = np.asarray(L0_ffn_down_codes).T, np.asarray(L0_ffn_down_scales).T
    d_c = np.concatenate([dc, dc[full * P:]]).reshape(full + 1, P, H)
    d_s = np.concatenate([ds, ds[2 * full:]]).reshape(full + 1, 2, H)

    arrays = {"x": x, "ctx": ctx, "gu_codes": np.stack(gu_c), "gu_scales": np.stack(gu_s),
              "d_codes": d_c, "d_scales": d_s}
    nc = bacc.Bacc("TRN2", target_bir_lowering=False, num_devices=1, dynamic_dma_scratch_size=1024)
    args, ins = [], {}
    for name, a in arrays.items():
        ins[f"in_{name}"] = np.ascontiguousarray(a)
        args.append(nc.dram_tensor(f"in_{name}", a.shape, mybir.dt.from_np(a.dtype), kind="ExternalInput").ap())
    out = nc.dram_tensor("out_y", x.shape, F32, kind="ExternalOutput").ap()
    xattn_ffn(nc, *args, out)
    r = run(nc, [ins], core_ids=[0])
    return r.results[0]["out_y"]
```

```python
from contextlib import ExitStack

import concourse.bass as bass
from concourse import mybir

F32 = mybir.dt.float32
F32R = mybir.dt.float32r
I32 = mybir.dt.int32
BF16 = mybir.dt.bfloat16
ALU = mybir.AluOpType
ACT = mybir.ActivationFunctionType
AX = mybir.AxisListType

P = 128
HEADS = 8
BLOCK = 64
EPS = 1e-5
WIDE = 512
XS = 4
LR = 4

LINES = [(0.30380716919898987, 1.1266502141952515), (0.1301555633544922, 0.12570476531982422),
         (0.09966795146465302, 0.014562471769750118), (0.09105003625154495, 0.0),
         (0.08134990185499191, -0.0017696022987365723), (0.09180294722318649, -0.02929653413593769),
         (0.12190717458724976, -0.16882604360580444), (0.2770431637763977, -1.2163453102111816)]
CENTRE = 7.0


class Batch:

    def __init__(self, p, j):
        self.n = p * XS + j
        self.xslot, self.xround = j % XS, p + j // XS
        self.slot, self.round = j % 2, p * (XS // 2) + j // 2


class Steps:

    def __init__(self, sem):
        self.sem, self.base, self.local = sem, 0, 0

    def mark(self, ins):
        ins.then_inc(self.sem, 1)
        self.local += 1
        return self.base + self.local

    def enter(self, p, per, first=0):
        start = self.base + self.local - first * per
        self.base, self.local, self.start, self.per = p * per + start, 0, start, per

    def leave(self, end):
        assert self.local == self.per, (self.local, self.per)
        self.base, self.local = self.start + end * self.per, 0


def wait(eng, sem, value):
    if not (isinstance(value, int) and value <= 0):
        eng.wait_ge(sem, value)


def xattn_ffn(nc, x, ctx, gu_codes, gu_scales, d_codes, d_scales, out):
    B, C, N = x.shape
    T = B * C
    GU = gu_codes.shape[0]
    KT = d_codes.shape[0]
    HT = N // P
    TB = T // WIDE
    TT = T // P
    HALF = P // 2
    QT = WIDE // P
    FULL = KT - 1
    ITEM = HT * P
    assert C == P and ITEM == N and GU == 2 * FULL + 1 and N == 2 * WIDE and T == TB * WIDE
    assert QT == XS and B % XS == 0 and B >= 2 * XS and FULL % 2 == 1 and TB == 4
    NI = GU + KT

    x1_dram = nc.dram_tensor("x1_scratch", (B, P, N), F32).ap()
    wd_dram = nc.dram_tensor("wd_scratch", (KT, P, N), F32).ap()
    inter_dram = nc.dram_tensor("inter_scratch", (TT, P, KT, P), F32).ap()

    with ExitStack() as st:
        def sb(name, shape, dt):
            return st.enter_context(nc.sbuf_tensor(name, shape, dt))

        def sem(name):
            return st.enter_context(nc.semaphore(name))

        with nc.sbuf_tensor("early1", [P, 2 * HT * T], F32) as early1, nc.sbuf_tensor("early2", [P, 8 * ITEM], F32) as early2:
            pass
        R1 = sb("R1", [P, 2 * HT * T], F32R)
        R2 = sb("R2", [P, 8 * ITEM], F32R)
        F = sb("F", [P, 15 * N], F32)
        ident = sb("ident", [P, P], F32)
        headmask = sb("headmask", [P, P], F32)
        headsel = sb("headsel", [P, HEADS], F32)
        halfneg = sb("halfneg", [P, 1], F32)
        one = sb("one", [P, 1], F32)
        eps = sb("eps", [P, 1], F32)
        bn = sb("bn", [P, 2, 6], F32)
        bn2 = sb("bn2", [P, 2, 6], F32)
        mv = sb("mv", [P, 2], F32)
        mv2 = sb("mv2", [P, 2], F32)
        credit = sb("credit", [P, 16], F32)
        veps = sb("veps", [P, 1], F32)
        veps2 = sb("veps2", [P, 1], F32)
        rstd = sb("rstd", [P, 1], F32)
        rstd2 = sb("rstd2", [P, 1], F32)
        nmr = sb("nmr", [P, 1], F32)
        nmr2 = sb("nmr2", [P, 1], F32)
        nkmax = sb("nkmax", [P, 1], F32)
        ksum = sb("ksum", [P, 1], F32)
        rksum = [sb(f"rksum{s}", [P, 1], F32) for s in range(2)]
        rden = sb("rden", [P, HT * HEADS], F32)
        kvs = sb("kvs", [P, P], F32)

        banks = [st.enter_context(nc.psum_tensor(f"bank{i}", [P, 2, WIDE], F32)) for i in range(4)]

        xh, xl = [R1[:, :].rearrange("p (b q t n) -> p b q t n", b=TB, q=2, t=HT)[:, :, q] for q in range(2)]
        wgu = R2[:, :].rearrange("p (s q g n) -> p s q g n", s=2, q=2, g=2)

        def f(i, n=1):
            return F[:, i * N:(i + n) * N]

        codes = [f(0).bitcast(I32), f(1).bitcast(I32)]
        scales = [f(2), f(3)]
        code7 = [f(4).bitcast(BF16)[:, s * N:(s + 1) * N] for s in range(2)]
        lines = [f(5 + i) for i in range(LR)]
        low, high = f(9), f(10)
        w = [f(11), f(12)]
        silu = [F[:, 13 * N + s * WIDE:13 * N + (s + 1) * WIDE] for s in range(2)]
        inter = [F[:, 14 * N + s * WIDE:14 * N + (s + 1) * WIDE] for s in range(2)]

        xs, cs = [f(13), f(9), f(0), f(12)], [f(14), f(1)]
        x1 = [f(2), f(3)]
        expq = [f(4), f(11)]
        expk, expkT, ctxT, rdenw, x2 = f(5), f(6), f(7), f(8), f(10)
        pCtxT, pAttn, pX2T = [banks[i][:, :, :].rearrange("p a n -> p (a n)") for i in (0, 2, 3)]
        pRdenT, pExpkT = pAttn, pCtxT
        pDen = banks[1][:, 0, 0:HT * HEADS]
        pKV = banks[1][:, 1, 0:P]

        SLICES = B // XS
        SL = N // SLICES
        assert 4 * N <= 2 * HT * WIDE and 7 * 2 * SL + SL <= 4 * ITEM
        at0 = 3 * 2 * HT * WIDE
        fcodes = early1[:, at0:at0 + 2 * N].bitcast(I32).rearrange("p (i n) -> p i n", i=2)
        fscales = early1[:, at0 + 2 * N:at0 + 4 * N].rearrange("p (i n) -> p i n", i=2)
        small = [early2[:, 4 * ITEM + i * 2 * SL:4 * ITEM + (i + 1) * 2 * SL].rearrange("p (i n) -> p i n", i=2) for i in range(7)]
        flines, flow, fhigh, fw = small[0:LR], small[LR], small[LR + 1], small[LR + 2]
        fcode7 = early2[:, 4 * ITEM + 14 * SL:4 * ITEM + 15 * SL].bitcast(BF16).rearrange("p (i n) -> p i n", i=2)

        HW = KT * WIDE
        IT = KT * P
        wdh, wdl = [R1[:, 0:2 * HW].rearrange("p (k q n) -> p k q n", k=KT, q=2)[:, :, q] for q in range(2)]
        WB = 2 * HT * WIDE // (2 * WIDE)
        ih = [R2[:, 0:IT], R1[:, 2 * HW:2 * HW + IT]]
        il = [R1[:, 2 * HW + IT:2 * HW + 2 * IT], R1[:, 2 * HW + 2 * IT:2 * HW + 3 * IT]]
        FS = 15
        rest = [IT, IT + WIDE, 5 * ITEM, 5 * ITEM + WIDE, 7 * ITEM, 7 * ITEM + WIDE, 4 * ITEM]
        stage = [F[:, k * WIDE:(k + 1) * WIDE] for k in range(FS)] + \
                [R2[:, a:a + WIDE].bitcast(F32) for a in rest]
        it = [F[:, FS * WIDE + s * IT:FS * WIDE + (s + 1) * IT] for s in range(2)]
        free = FS * WIDE + 2 * IT
        xo = [F[:, free + s * WIDE:free + (s + 1) * WIDE] for s in range(2)]
        yo = [F[:, free + (2 + s) * WIDE:free + (3 + s) * WIDE] for s in range(2)]
        assert 2 * HW + 3 * IT <= 2 * HT * T and IT + 2 * WIDE <= 4 * ITEM and FS + len(rest) == KT
        assert free >= 13 * N and free + 4 * WIDE <= 15 * N and IT <= 4 * ITEM
        GROUPS = [(0, 4), (4, 8), (8, 12), (12, FS), (FS, FS + 2), (FS + 2, FS + 4), (FS + 4, FS + 6), (FS + 6, KT)]

        consts_ready = sem("consts_ready")
        x_in = [sem(f"x_in{s}") for s in range(XS)]
        ctx_in = [sem(f"ctx_in{s}") for s in range(2)]
        x1_free = [sem(f"x1_free{s}") for s in range(2)]
        veps_ready, veps2_ready = sem("veps_ready"), sem("veps2_ready")
        mv_ready, rstd_ready, nmr_ready = sem("mv_ready"), sem("rstd_ready"), sem("nmr_ready")
        mv2_ready, rstd2_ready, nmr2_ready = sem("mv2_ready"), sem("rstd2_ready"), sem("nmr2_ready")
        kmax_ready, expq_ready, expk_ready = sem("kmax_ready"), sem("expq_ready"), sem("expk_ready")
        ctx_turned, ctxT_ready = sem("ctx_turned"), sem("ctxT_ready")
        expk_turned, expkT_ready = sem("expk_turned"), sem("expkT_ready")
        den_done, rden_ready, rdenw_ready = sem("den_done"), sem("rden_ready"), sem("rdenw_ready")
        rksum_ready, rden_turned = sem("rksum_ready"), sem("rden_turned")
        kv_done, kvs_ready, softq_ready = sem("kv_done"), sem("kvs_ready"), sem("softq_ready")
        attn_done, x1_ready, x2_ready = sem("attn_done"), sem("x1_ready"), sem("x2_ready")
        x2_turned, xh_ready, xl_ready = sem("x2_turned"), sem("xh_ready"), sem("xl_ready")
        fcodes_in, fscales_in, fcode7_ready = sem("fcodes_in"), sem("fscales_in"), sem("fcode7_ready")
        fline_ready, fmerged, fsum_ready = sem("fline_ready"), sem("fmerged"), sem("fsum_ready")
        fw_ready, fwh_ready, fwl_ready = sem("fw_ready"), sem("fwh_ready"), sem("fwl_ready")
        codes_in = [sem(f"codes_in{s}") for s in range(2)]
        scales_in = [sem(f"scales_in{s}") for s in range(2)]
        code7_ready, line_ready, lines_merged = sem("code7_ready"), sem("line_ready"), sem("lines_merged")
        w_ready, wh_ready, wl_ready = sem("w_ready"), sem("wh_ready"), sem("wl_ready")
        wd_stored = [sem(f"wd_stored{s}") for s in range(2)]
        gate_done, up_done, silu_ready = sem("gate_done"), sem("up_done"), sem("silu_ready")
        blocks_done = sem("blocks_done")
        up_copied = sem("up_copied")
        inter_stored = [sem(f"inter_stored{s}") for s in range(2)]
        stage_in = [sem(f"stage_in{g}") for g in range(len(GROUPS))]
        wdh_ready, wdl_ready = sem("wdh_ready"), sem("wdl_ready")
        inter_in = [sem(f"inter_in{s}") for s in range(2)]
        late_in = [sem(f"late_in{s}") for s in range(2)]
        x1_in = [sem(f"x1_in{s}") for s in range(2)]
        ih_ready, il_ready = sem("ih_ready"), sem("il_ready")
        ih_first, il_first = sem("ih_first"), sem("il_first")
        down_step, y_ready = sem("down_step"), sem("y_ready")
        y_stored = [sem(f"y_stored{s}") for s in range(2)]
        dve_step = sem("dve_step")
        pool_step = sem("pool_step")

        NCONST = 3
        LOOPS = B // XS - 1
        PAIRS = FULL // 2
        TILES = 2 * TT

        def batch(p, k, d):
            if isinstance(p, int) and not 0 <= p * XS + k - d < B:
                return None
            return Batch(p, k - d)

        def mixer(engine, turn, stages):
            for k in range(XS):
                turn(0, k)
            with engine.Fori(0, LOOPS) as p:
                for k in range(XS, 2 * XS):
                    turn(p, k)
            for k in range(XS, XS + stages - 1):
                turn(LOOPS, k)

        def tokens_of(v, b):
            cols = slice(b.xslot * P, (b.xslot + 1) * P)
            if isinstance(b.n, int):
                return v[:, b.xround, :, cols]
            return v[:, bass.ds(b.xround, 1), :, cols].rearrange("p o t n -> p (o t) n")

        def slice_at(p, k):
            g = p + k // XS
            return (None if isinstance(g, int) and g >= SLICES else g), k % XS

        def columns(v, g):
            return v[:, :, g * SL:(g + 1) * SL] if isinstance(g, int) else v[:, :, bass.ds(g * SL, SL)]

        block = st.enter_context(nc.Block())

        @block.sync
        def _(sp):
            def load_codes(slot, src):
                sp.dma_start(codes[slot], src).then_inc(codes_in[slot], 16)

            def load_scales(slot, src):
                sp.dma_start(scales[slot], src.unsqueeze(1).to_broadcast([2, BLOCK, ITEM])).then_inc(scales_in[slot], 16)

            def at(a, i):
                return a[i] if isinstance(i, int) else a[bass.ds(i, 1)].rearrange("o p n -> (o p) n")

            def load_item(n, slot, cod, scl, i):
                wait(sp, code7_ready, n - 1)
                load_codes(slot, at(cod, i))
                wait(sp, w_ready, n - 1)
                load_scales(slot, at(scl, i))

            def load_x(b):
                sp.dma_start(xs[b.xslot], at(x, b.n)).then_inc(x_in[b.xslot], 16)

            def load_ctx(b):
                sp.dma_start(cs[b.slot], at(ctx, b.n)).then_inc(ctx_in[b.slot], 16)

            def mixer_turn(p, k):
                b, old = batch(p, k, 0), batch(p, k, XS)
                if old:
                    sp.wait_ge(x1_ready, old.n + 1)
                if b and batch(p, k, 2):
                    load_x(b)
                    sp.wait_ge(ctx_turned, b.n - 1)
                    sp.wait_ge(expk_ready, b.n - 1)
                    load_ctx(b)
                if old:
                    sp.dma_start(at(x1_dram, old.n), x1[old.slot]).then_inc(x1_free[old.slot], 16)

            load_x(Batch(0, 0))
            load_ctx(Batch(0, 0))
            sp.dma_start(fcodes, gu_codes[0:2].rearrange("i p n -> p i n")).then_inc(fcodes_in, 16)
            load_x(Batch(0, 1))
            load_ctx(Batch(0, 1))
            for i in range(2):
                sp.dma_start(fscales[:, i, :], gu_scales[i].unsqueeze(1).to_broadcast([2, BLOCK, ITEM])).then_inc(fscales_in, 16)
            mixer(sp, mixer_turn, XS)
            load_codes(0, d_codes[0])
            sp.wait_ge(ctx_turned, B)
            sp.wait_ge(expk_ready, B)
            load_codes(1, gu_codes[2])
            sp.wait_ge(x1_free[0], 16 + B // 2 * 16)
            sp.wait_ge(x2_ready, B - 1)
            load_scales(0, d_scales[0])
            mixer_turn(LOOPS, 2 * XS - 1)
            sp.wait_ge(x1_free[1], 16 + B // 2 * 16)
            sp.wait_ge(x2_ready, B)
            load_scales(1, gu_scales[2])

            def store_block(c, tb, rows=None):
                s = tb % 2
                sp.wait_ge(blocks_done, c * TB + tb + 1 + TB)
                if rows is None:
                    dst = inter_dram[tb * QT:(tb + 1) * QT, :, bass.ds(c, 1), :].rearrange("q p o n -> p (q o) n")
                    sp.dma_start(dst, inter[s].rearrange("p (q n) -> p q n", q=QT)).then_inc(inter_stored[s], 16)
                    return
                for a in range(2):
                    dst = inter_dram[tb * QT:(tb + 1) * QT, a * HALF:(a + 1) * HALF, c, :].rearrange("q p n -> p q n")
                    sp.dma_start(dst, inter[s][0:HALF, :].rearrange("p (q n) -> p q n", q=QT)).then_inc(inter_stored[s], 16)

            def store_wd(c, par):
                sp.wait_ge(w_ready, c * 3 + 3)
                sp.dma_start(at(wd_dram, c), w[par]).then_inc(wd_stored[par], 16)

            with sp.Fori(0, PAIRS) as p:
                for j in range(2):
                    c = p * 2 + j
                    n = p * 6 + 2 + 3 * j
                    load_item(n + 2, j, gu_codes, gu_scales, c * 2 + 3)
                    store_wd(c, j)
                    store_block(c, 0)
                    load_item(n + 3, 1 - j, d_codes, d_scales, c + 1)
                    store_block(c, 1)
                    load_item(n + 4, j, gu_codes, gu_scales, c * 2 + 4)
                    store_block(c, 2)
                    store_block(c, 3)

            def load_stage(half, g):
                a, b = GROUPS[g]
                src = wd_dram[a:b, :, half * WIDE:(half + 1) * WIDE].rearrange("k p n -> p k n")
                if a < FS:
                    dst = F[:, a * WIDE:b * WIDE].rearrange("p (k n) -> p k n", n=WIDE)
                else:
                    r = rest[a - FS]
                    dst = R2[:, r:r + (b - a) * WIDE].bitcast(F32).rearrange("p (k n) -> p k n", n=WIDE)
                sp.dma_start(dst, src).then_inc(stage_in[g], 16)

            def load_tile(t, slot, half, cols=(0, KT)):
                g = t + half * TT
                wait(sp, il_ready, g - 1)
                a, b = cols
                dst = it[slot][:, a * P:b * P].rearrange("p (k n) -> p k n", n=P)
                src = inter_dram[t] if isinstance(t, int) else \
                    inter_dram[bass.ds(t, 1)].rearrange("o p k n -> (o p) k n")
                sp.dma_start(dst, src[:, a:b, :]).then_inc(inter_in[slot], 16)

            c = FULL - 1
            load_item(NI - 1, 0, d_codes, d_scales, KT - 1)
            store_wd(c, c % 2)
            store_block(c, 0)
            store_block(c, 1)
            sp.wait_ge(code7_ready, NI)
            sp.wait_ge(wd_stored[0], 16 * (FULL // 2 + 1))
            sp.wait_ge(wd_stored[1], 16 * (FULL // 2))
            load_stage(0, 0)
            sp.wait_ge(w_ready, NI)
            sp.dma_start(wd_dram[KT - 1], w[0]).then_inc(wd_stored[0], 16)
            load_stage(0, 1)
            store_block(c, 2)
            load_stage(0, 2)
            sp.wait_ge(wd_stored[0], 16 * (FULL // 2 + 2))
            for s in range(2):
                sp.wait_ge(inter_stored[s], 16 * 2 * FS)
            load_tile(0, 0, 0, (0, FS))
            store_block(c, 3)
            load_stage(0, 3)
            store_block(FULL, 0, HALF)
            load_tile(1, 1, 0, (0, FS))
            store_block(FULL, 1, HALF)
            sp.wait_ge(up_done, FULL * TB)
            load_stage(0, 4)
            load_stage(0, 5)
            store_block(FULL, 2, HALF)
            load_stage(0, 6)
            store_block(FULL, 3, HALF)
            sp.wait_ge(gate_done, TB * KT)
            load_stage(0, 7)
            for s in range(2):
                sp.wait_ge(inter_stored[s], 16 * (2 * FULL + 4))
            for t in range(2):
                sp.dma_start(it[t][:, FS * P:].rearrange("p (k n) -> p k n", n=P),
                             inter_dram[t, :, FS:, :]).then_inc(late_in[t], 16)

            def load_x1(t, slot, half):
                sp.dma_start(xo[slot], at(x1_dram, t)[:, half * WIDE:(half + 1) * WIDE]).then_inc(x1_in[slot], 16)

            def store_y(t, slot, half):
                sp.wait_ge(y_ready, t + half * TT + 1)
                sp.dma_start(at(out, t)[:, half * WIDE:(half + 1) * WIDE], yo[slot]).then_inc(y_stored[slot], 16)

            def tile_pair(q, half):
                for s in range(2):
                    t = q * 2 + s
                    load_tile(t, s, half)
                    store_y(t - 2, s, half)
                    load_x1(t, s, half)

            for half in range(2):
                for t in range(2):
                    if half:
                        load_tile(t, t, half)
                        store_y(TT - 2 + t, t, half - 1)
                    load_x1(t, t, half)
                tile_pair(1, half)
                if half == 0:
                    for g in range(len(GROUPS)):
                        load_stage(1, g)
                with sp.Fori(2, TT // 2) as q:
                    tile_pair(q, half)
            for s in range(2):
                store_y(TT - 2 + s, s, 1)
            for s in range(2):
                sp.wait_ge(y_stored[s], 16 * TT)

        @block.gpsimd
        def _(pool):
            own = Steps(pool_step)
            m = [own.mark(nc.gpsimd.memset(a, v)) for a, v in
                 ((ident[:, :], 0.0), (headmask[:, :], 1.0), (headsel[:, :], 1.0), (halfneg[:, :], -0.5), (one[:, :], 1.0), (eps[:, :], EPS))]
            pool.wait_ge(pool_step, m[-1])
            nc.gpsimd.affine_select(out=ident[:, :], in_=ident[:, :], compare_op=ALU.not_equal, fill=1.0, base=0,
                                    pattern=[[-1, P]], channel_multiplier=1).then_inc(consts_ready, 1)
            D = P // HEADS
            for a, cols in ((headmask[:, :].rearrange("p (h d) -> p h d", h=HEADS), D), (headsel[:, :].unsqueeze(2), 1)):
                k = own.mark(nc.gpsimd.affine_select(out=a, in_=a, compare_op=ALU.is_ge, fill=0.0, base=0,
                                                     pattern=[[-D, HEADS], [0, cols]], channel_multiplier=1))
                pool.wait_ge(pool_step, k)
                nc.gpsimd.affine_select(out=a, in_=a, compare_op=ALU.is_ge, fill=0.0, base=D - 1,
                                        pattern=[[D, HEADS], [0, cols]], channel_multiplier=-1).then_inc(consts_ready, 1)

            def inverse_root(mv_ready, n, dst, mid, src, mid_ready, ready):
                pool.wait_ge(mv_ready, n + 1)
                nc.gpsimd.tensor_tensor(mid, src, eps[:, :], ALU.add).then_inc(mid_ready, 1)
                pool.wait_ge(mid_ready, n + 1)
                nc.gpsimd.tensor_tensor(dst, mid, halfneg[:, :], ALU.pow).then_inc(ready, 1)

            def mixer_turn(p, k):
                a, b, c = batch(p, k, 0), batch(p, k, 3), batch(p, k, 1)
                g, j = slice_at(p, k)
                if a:
                    wait(pool, expq_ready, a.n)
                    inverse_root(mv_ready, a.n, rstd[:, :], veps[:, :], mv[:, 1:2], veps_ready, rstd_ready)
                if g is not None and j == XS - 1:
                    pool.wait_ge(fmerged, g * 6 + 6)
                    wait(pool, fwh_ready, g)
                    nc.gpsimd.tensor_tensor(fw, fhigh, flow, ALU.add).then_inc(fsum_ready, 1)
                if b:
                    wait(pool, x2_ready, b.n)
                    inverse_root(mv2_ready, b.n, rstd2[:, :], veps2[:, :], mv2[:, 1:2], veps2_ready, rstd2_ready)
                if g is not None and j == XS - 1:
                    pool.wait_ge(fscales_in, 32)
                    pool.wait_ge(fsum_ready, g + 1)
                    nc.gpsimd.tensor_tensor(fw, fw, columns(fscales, g), ALU.mult).then_inc(fw_ready, 1)
                if j == 0 and not (isinstance(p, int) and p * XS + k == 0):
                    h = p + k // XS - 1
                    pool.wait_ge(fwh_ready, h + 1)
                    nc.gpsimd.tensor_tensor(columns(wgu[:, 0, 1], h), fw, columns(wgu[:, 0, 0], h).bitcast(F32),
                                            ALU.subtract).then_inc(fwl_ready, 1)
                if c:
                    pool.wait_ge(rden_ready, c.n + 1)
                    wait(pool, rden_turned, c.n)
                    nc.gpsimd.tensor_tensor(rdenw.rearrange("p (t d) -> p t d", d=D),
                                            rden[:, :].unsqueeze(2).to_broadcast([P, HT * HEADS, D]),
                                            one[:, :].unsqueeze(2).to_broadcast([P, HT * HEADS, D]),
                                            ALU.mult).then_inc(rdenw_ready, 1)

            mixer(pool, mixer_turn, 4)

        def lines_of(act, n, s, middle=None):
            act.wait_ge(code7_ready, n + 1)
            for q in range(8):
                if q < LR:
                    wait(act, lines_merged, (n - 1) * 6 + [4, 4, 5, 6][q])
                else:
                    act.wait_ge(lines_merged, n * 6 + [1, 1, 2, 3][q - LR])
                slope, offset = LINES[q]
                nc.scalar.activation(lines[q % LR], code7[s], ACT.Copy, bias=offset, scale=slope).then_inc(line_ready, 1)
                if q == LR - 1 and middle:
                    middle()

        @block.scalar
        def _(act):
            def hi_of(n, s, c, g, par):
                act.wait_ge(w_ready, n + 1)
                wait(act, up_done, (c - 1) * TB)
                nc.scalar.activation(wgu[:, par, 0, g], w[s], ACT.Copy).then_inc(wh_ready, 1)

            def flines_of(g, qs):
                if 0 in qs:
                    act.wait_ge(fcodes_in, 16)
                    nc.scalar.activation(fcode7, columns(fcodes, g), ACT.Copy, bias=-CENTRE).then_inc(fcode7_ready, 1)
                act.wait_ge(fcode7_ready, g + 1)
                for q in qs:
                    wait(act, fmerged, (g - 1) * 6 + [4, 4, 5, 6][q] if q < LR else g * 6 + [1, 1, 2, 3][q - LR])
                    slope, offset = LINES[q]
                    nc.scalar.activation(flines[q % LR], fcode7, ACT.Copy, bias=offset, scale=slope).then_inc(fline_ready, 1)

            def mixer_turn(p, k):
                a, b, c = batch(p, k, 0), batch(p, k, 3), batch(p, k, 2)
                g, j = slice_at(p, k)
                if a:
                    act.wait_ge(nmr_ready, a.n + 1)
                    wait(act, attn_done, a.n - 1)
                    nc.scalar.activation(expq[a.slot], xs[a.xslot], ACT.Exp, bias=nmr[:, :], scale=rstd[:, :]).then_inc(expq_ready, 1)
                    act.wait_ge(kmax_ready, a.n + 1)
                    wait(act, expk_turned, a.n)
                    wait(act, rksum_ready, a.n)
                    nc.scalar.activation(expk, cs[a.slot], ACT.Exp, bias=nkmax[:, :], accum_out=ksum[:, :]).then_inc(expk_ready, 1)
                if g is not None and j == 0:
                    flines_of(g, range(LR))
                if g is not None and j == 1:
                    flines_of(g, range(LR, 8))
                if g is not None and j == XS - 1:
                    act.wait_ge(fw_ready, g + 1)
                    nc.scalar.activation(columns(wgu[:, 0, 0], g), fw, ACT.Copy).then_inc(fwh_ready, 1)
                if b:
                    act.wait_ge(x2_turned, b.n + 1)
                    nc.scalar.copy(tokens_of(xh, b), pX2T.rearrange("p (t n) -> p t n", t=HT)).then_inc(xh_ready, 1)
                if a:
                    act.wait_ge(ctx_turned, a.n + 1)
                    wait(act, kv_done, a.n)
                    nc.scalar.copy(ctxT, pCtxT).then_inc(ctxT_ready, 1)
                    act.wait_ge(expk_turned, a.n + 1)
                    nc.scalar.copy(expkT, pExpkT).then_inc(expkT_ready, 1)
                if c:
                    act.wait_ge(nmr2_ready, c.n + 1)
                    nc.scalar.activation(x2, x1[c.slot], ACT.Identity, bias=nmr2[:, :], scale=rstd2[:, :]).then_inc(x2_ready, 1)

            mixer(act, mixer_turn, 2)

            def silu_of(c, tb):
                act.wait_ge(gate_done, c * TB + tb + 1)
                act.wait_ge(blocks_done, c * TB + tb - 1 + TB)
                nc.scalar.activation(silu[tb % 2], banks[tb][:, 0, :], ACT.Silu).then_inc(silu_ready, 1)

            def chunk_pair(p, first=0):
                for j in range(2):
                    c = p * 2 + j
                    n = p * 6 + 2 + 3 * j
                    if j >= first:
                        lines_of(act, n, j)
                    silu_of(c, 0)
                    lines_of(act, n + 1, 1 - j)
                    silu_of(c, 1)
                    lines_of(act, n + 2, j, lambda: hi_of(n + 1, 1 - j, c + 1, 0, 1 - j))
                    hi_of(n + 2, j, c + 1, 1, 1 - j)
                    silu_of(c, 2)
                    silu_of(c, 3)

            def last_turns():
                mixer_turn(LOOPS, XS + 1)
                mixer_turn(LOOPS, XS + 2)

            act.wait_ge(kv_done, B)
            act.wait_ge(rden_turned, B)
            lines_of(act, 2, 0, last_turns)
            chunk_pair(0, 1)
            with act.Fori(1, PAIRS) as p:
                chunk_pair(p)
            c = FULL - 1
            lines_of(act, NI - 3, 0)
            silu_of(c, 0)
            lines_of(act, NI - 2, 1)
            hi_of(NI - 2, 1, FULL, 0, 1)
            silu_of(c, 1)
            lines_of(act, NI - 1, 0)
            silu_of(c, 2)
            silu_of(c, 3)

            def last_block(tb):
                s = tb % 2
                act.wait_ge(gate_done, FULL * TB + tb + 1)
                act.wait_ge(blocks_done, FULL * TB + tb - 1 + TB)
                nc.scalar.activation(silu[s][0:HALF, :], banks[tb][0:HALF, 0, :], ACT.Silu).then_inc(silu_ready, 1)
                act.wait_ge(inter_stored[s], 16 * (2 * FULL + 2 * (tb // 2)))
                nc.scalar.copy(inter[s][0:HALF, :], banks[tb][HALF:P, 0, :]).then_inc(up_copied, 1)

            def split_weights(half, a=0, b=KT):
                for k in range(a, b):
                    for g, (start, _) in enumerate(GROUPS):
                        if start == k:
                            act.wait_ge(stage_in[g], 16 * (half + 1))
                    if half:
                        act.wait_ge(down_step, KT * (TT - 1) + k + 1)
                    nc.scalar.copy(wdh[:, k, :], stage[k]).then_inc(wdh_ready, 1)

            def split_tile(g, slot, uses):
                act.wait_ge(inter_in[slot], uses)
                wait(act, down_step, (g - 1) * KT)
                nc.scalar.copy(ih[slot], it[slot]).then_inc(ih_ready, 1)

            last_block(0)
            split_weights(0, 0, WB // 2)
            last_block(1)
            split_weights(0, WB // 2, WB + WB // 2)
            last_block(2)
            act.wait_ge(inter_in[0], 16)
            act.wait_ge(up_done, FULL * TB)
            nc.scalar.copy(ih[0][:, 0:FS * P], it[0][:, 0:FS * P]).then_inc(ih_first, 1)
            last_block(3)
            split_weights(0, WB + WB // 2, FS)
            act.wait_ge(inter_in[1], 16)
            nc.scalar.copy(ih[1][:, 0:FS * P], it[1][:, 0:FS * P]).then_inc(ih_first, 1)
            split_weights(0, FS, KT)
            for t in range(2):
                act.wait_ge(late_in[t], 16)
                nc.scalar.copy(ih[t][:, FS * P:], it[t][:, FS * P:]).then_inc(ih_ready, 1)
            for half in range(2):
                g0, u0 = half * TT, 16 * half * TT // 2
                if half:
                    split_tile(g0, 0, u0 + 16)
                    split_weights(half)
                    split_tile(g0 + 1, 1, u0 + 16)
                with act.Fori(0, TT // 2 - 1) as q:
                    for s in range(2):
                        split_tile(q * 2 + (g0 + 2 + s), s, q * 16 + (u0 + 32))

        @block.vector
        def _(dve):
            own = Steps(dve_step)

            def after(token):
                dve.wait_ge(dve_step, token)

            for i in range(TB):
                nc.vector.memset(credit[:, i:i + 1], 0.0).then_inc(blocks_done, 1)
            for s in range(2):
                nc.vector.memset(credit[:, TB + s:TB + s + 1], 0.0).then_inc(x1_free[s], 16)

            def centre(s, uses):
                dve.wait_ge(codes_in[s], uses)
                nc.vector.tensor_scalar(code7[s], codes[s], CENTRE, None, ALU.subtract).then_inc(code7_ready, 1)

            def merge(n, s, uses, middle=None, w_free=None):
                at = lambda q: lines[q % LR]
                vt = nc.vector
                dve.wait_ge(line_ready, n * 8 + 2)
                vt.scalar_tensor_tensor(low, at(0), 0.0, at(1), ALU.min, ALU.min).then_inc(lines_merged, 1)
                for q in (2, 3):
                    dve.wait_ge(line_ready, n * 8 + q + 1)
                    dve.wait_ge(lines_merged, n * 6 + q - 1)
                    vt.tensor_tensor(low, low, at(q), ALU.min).then_inc(lines_merged, 1)
                if middle:
                    middle()
                dve.wait_ge(line_ready, n * 8 + 6)
                vt.tensor_tensor(high, at(4), at(5), ALU.max).then_inc(lines_merged, 1)
                for q in (6, 7):
                    dve.wait_ge(line_ready, n * 8 + q + 1)
                    dve.wait_ge(lines_merged, n * 6 + q - 2)
                    vt.tensor_tensor(high, high, at(q), ALU.max).then_inc(lines_merged, 1)
                if w_free:
                    dve.wait_ge(*w_free)
                dve.wait_ge(lines_merged, n * 6 + 6)
                after(own.mark(vt.scalar_tensor_tensor(w[s], high, 0.0, low, ALU.max, ALU.add)))
                dve.wait_ge(scales_in[s], uses)
                vt.tensor_tensor(w[s], w[s], scales[s], ALU.mult).then_inc(w_ready, 1)

            def lo_of(m, s, g, par):
                dve.wait_ge(wh_ready, m + 1)
                nc.vector.tensor_tensor(wgu[:, par, 1, g], w[s], wgu[:, par, 0, g].bitcast(F32), ALU.subtract).then_inc(wl_ready, 1)

            for i, (count, n) in enumerate(((code7_ready, 2), (line_ready, 16), (lines_merged, 12), (w_ready, 2), (wh_ready, 2),
                                            (wl_ready, 2), (codes_in[0], 16), (codes_in[1], 16), (scales_in[0], 16), (scales_in[1], 16))):
                nc.vector.memset(credit[:, TB + 2 + i:TB + 3 + i], 0.0).then_inc(count, n)

            def stats(src, bn_, mv_, ready):
                for i in range(2):
                    nc.vector.bn_stats(bn_[:, i, :], src[:, i * WIDE:(i + 1) * WIDE])
                dve.drain()
                nc.vector.bn_aggr(mv_[:, :], bn_[:, :, :].rearrange("p a n -> p (a n)")).then_inc(ready, 1)

            def fmerge(g, j, i):
                if g is None or j not in (1, 2):
                    return
                dst, op = (flow, ALU.min) if j == 1 else (fhigh, ALU.max)
                dve.wait_ge(fline_ready, g * 8 + (j - 1) * LR + i + 2)
                if i == 0:
                    wait(dve, fsum_ready, g)
                    m = nc.vector.scalar_tensor_tensor(dst, flines[0], 0.0, flines[1], op, op)
                else:
                    dve.wait_ge(fmerged, g * 6 + (j - 1) * 3 + i)
                    m = nc.vector.tensor_tensor(dst, dst, flines[i + 1], op)
                m.then_inc(fmerged, 1)

            def mixer_turn(p, k):
                a, b, c, d, e = [batch(p, k, i) for i in range(5)]
                g, j = slice_at(p, k)
                if a:
                    dve.wait_ge(x_in[a.xslot], (a.xround + 1) * 16)
                    stats(xs[a.xslot], bn, mv, mv_ready)
                if d:
                    dve.wait_ge(attn_done, d.n + 1)
                    dve.wait_ge(x1_free[d.slot], (d.round + 1) * 16)
                    nc.vector.tensor_tensor(x1[d.slot], xs[d.xslot], pAttn, ALU.add).then_inc(x1_ready, 1)
                    dve.wait_ge(x1_ready, d.n + 1)
                    stats(x1[d.slot], bn2, mv2, mv2_ready)
                if a:
                    dve.wait_ge(rstd_ready, a.n + 1)
                    nc.vector.scalar_tensor_tensor(nmr[:, :], mv[:, 0:1], -1.0, rstd[:, :], ALU.mult, ALU.mult).then_inc(nmr_ready, 1)
                if c:
                    dve.wait_ge(kv_done, c.n + 1)
                    dve.wait_ge(rksum_ready, c.n + 1)
                    nc.vector.scalar_tensor_tensor(kvs[:, :], pKV, rksum[c.slot][:, :], headmask[:, :], ALU.mult, ALU.mult).then_inc(kvs_ready, 1)
                if b:
                    dve.wait_ge(expk_ready, b.n + 1)
                    nc.vector.reciprocal(rksum[b.slot][:, :], ksum[:, :]).then_inc(rksum_ready, 1)
                if c:
                    dve.wait_ge(rden_turned, c.n + 1)
                    nc.vector.tensor_tensor(expq[c.slot], expq[c.slot], pRdenT, ALU.mult).then_inc(softq_ready, 1)
                fmerge(g, j, 0)
                if a:
                    dve.wait_ge(ctx_in[a.slot], (a.round + 1) * 16)
                    nc.vector.tensor_reduce(nkmax[:, :], cs[a.slot], AX.X, ALU.max, negate=True).then_inc(kmax_ready, 1)
                if d:
                    dve.wait_ge(rstd2_ready, d.n + 1)
                    nc.vector.scalar_tensor_tensor(nmr2[:, :], mv2[:, 0:1], -1.0, rstd2[:, :], ALU.mult, ALU.mult).then_inc(nmr2_ready, 1)
                fmerge(g, j, 1)
                if e:
                    dve.wait_ge(xh_ready, e.n + 1)
                    h, l = (tokens_of(v, e) for v in (xh, xl))
                    nc.vector.tensor_tensor(l, pX2T.rearrange("p (t n) -> p t n", t=HT), h.bitcast(F32), ALU.subtract).then_inc(xl_ready, 1)
                if b:
                    dve.wait_ge(den_done, b.n + 1)
                    nc.vector.reciprocal(rden[:, :], pDen).then_inc(rden_ready, 1)
                fmerge(g, j, 2)

            dve.wait_ge(consts_ready, NCONST)
            mixer(dve, mixer_turn, 3)

            def block_out(c, tb):
                dve.wait_ge(silu_ready, c * TB + tb + 1)
                dve.wait_ge(up_done, c * TB + tb + 1)
                wait(dve, inter_stored[tb % 2], c * 32 + 16 * (tb // 2))
                nc.vector.tensor_tensor(inter[tb % 2], silu[tb % 2], banks[tb][:, 1, :], ALU.mult).then_inc(blocks_done, 1)

            centre(0, 32)
            mixer_turn(LOOPS, XS + 2)

            def chunk_pair(p):
                for j in range(2):
                    c = p * 2 + j
                    n = p * 6 + 2 + 3 * j

                    def uses(i):
                        return p * 48 + 16 * ((2 + 3 * j + i) // 2 + 1)

                    def after_low():
                        if isinstance(n, int) and n == 2:
                            mixer_turn(LOOPS, XS + 3)
                        centre(1 - j, uses(1))

                    def after_low_3():
                        dve.wait_ge(w_ready, n + 2)
                        lo_of(c * 2 + 2, 1 - j, 0, 1 - j)
                        centre(1 - j, uses(3))

                    merge(n, j, uses(0), after_low)
                    block_out(c, 0)
                    merge(n + 1, 1 - j, uses(1), lambda: centre(j, uses(2)))
                    block_out(c, 1)
                    merge(n + 2, j, uses(2), after_low_3, (wd_stored[j], p * 16 + 16))
                    dve.wait_ge(w_ready, n + 3)
                    lo_of(c * 2 + 3, j, 1, 1 - j)
                    block_out(c, 2)
                    block_out(c, 3)

            chunk_pair(0)
            with dve.Fori(1, PAIRS) as p:
                own.enter(p, 6, first=1)
                chunk_pair(p)
            own.leave(PAIRS)

            c = FULL - 1

            def loads(n):
                return 16 * (n // 2 + 1)

            merge(NI - 3, 0, loads(NI - 3), lambda: centre(1, loads(NI - 2)))
            block_out(c, 0)
            merge(NI - 2, 1, loads(NI - 2), lambda: centre(0, loads(NI - 1)))
            dve.wait_ge(w_ready, NI - 1)
            lo_of(2 * FULL, 1, 0, 1)
            block_out(c, 1)
            merge(NI - 1, 0, loads(NI - 1), None, (wd_stored[0], 16 * (FULL // 2 + 1)))
            block_out(c, 2)
            block_out(c, 3)

            def last_block(tb):
                s = tb % 2
                dve.wait_ge(silu_ready, FULL * TB + tb + 1)
                dve.wait_ge(up_copied, tb + 1)
                nc.vector.tensor_tensor(inter[s][0:HALF, :], inter[s][0:HALF, :], silu[s][0:HALF, :], ALU.mult).then_inc(blocks_done, 1)

            def split_weights(half, a=0, b=KT):
                for k in range(a, b):
                    dve.wait_ge(wdh_ready, half * KT + k + 1)
                    nc.vector.tensor_tensor(wdl[:, k, :], stage[k], wdh[:, k, :].bitcast(F32), ALU.subtract).then_inc(wdl_ready, 1)

            def lo_of_tile(slot, a=0, b=FULL):
                cols = slice(a * P, b * P)
                return nc.vector.tensor_tensor(il[slot][:, cols], it[slot][:, cols], ih[slot].bitcast(F32)[:, cols], ALU.subtract)

            def lo_last(slot):
                h = ih[slot].bitcast(F32)
                nc.vector.tensor_tensor(ih[slot][HALF:P, FULL * P:], it[slot][HALF:P, FULL * P:], h[HALF:P, FULL * P:],
                                        ALU.subtract).then_inc(il_ready, 1)

            def split_tile(g, slot):
                dve.wait_ge(ih_ready, g + 1)
                lo_of_tile(slot)
                lo_last(slot)

            def tile_out(g, slot, uses):
                dve.wait_ge(down_step, (g + 1) * KT)
                dve.wait_ge(x1_in[slot], uses)
                wait(dve, y_stored[slot], uses - 16)
                nc.vector.tensor_tensor(yo[slot], xo[slot], banks[slot][:, 0, :], ALU.add).then_inc(y_ready, 1)

            for tb, (a, b) in enumerate(((0, WB // 2), (WB // 2, WB + WB // 2), (0, 0), (WB + WB // 2, FS))):
                last_block(tb)
                split_weights(0, a, b)
            for t in range(2):
                dve.wait_ge(ih_first, t + 1)
                lo_of_tile(t, 0, FS).then_inc(il_first, 1)
            split_weights(0, FS, KT)
            for half in range(2):
                g0 = half * TT
                if half:
                    split_tile(g0, 0)
                    split_weights(half)
                    tile_out(g0 - 1, 1, 16 * (TT // 2))
                    split_tile(g0 + 1, 1)
                else:
                    for t in range(2):
                        dve.wait_ge(ih_ready, t + 1)
                        lo_of_tile(t, FS)
                        lo_last(t)
                tile_out(g0, 0, 16 * (half * TT // 2 + 1))
                split_tile(g0 + 2, 0)
                tile_out(g0 + 1, 1, 16 * (half * TT // 2 + 1))
                with dve.Fori(0, TT // 2 - 2) as q:
                    for s in range(2):
                        g = q * 2 + (g0 + 3 + s)
                        split_tile(g, 1 - s)
                        tile_out(g - 1, s, q * 16 + 16 * (half * TT // 2 + 2))
                split_tile(g0 + TT - 1, 1)
                tile_out(g0 + TT - 2, 0, 16 * (half + 1) * TT // 2)
            tile_out(TILES - 1, 1, 16 * TT)

        @block.tensor
        def _(pe):
            def turn_tiles(dst, src):
                for t in range(HT):
                    i = pe.transpose(dst[:, t * P:(t + 1) * P], src[:, t * P:(t + 1) * P], ident[:, :])
                return i

            def mixer_turn(p, k):
                a, b, c = [batch(p, k, i) for i in range(3)]
                if a:
                    pe.wait_ge(ctx_in[a.slot], (a.round + 1) * 16)
                    wait(pe, expkT_ready, a.n)
                    turn_tiles(pCtxT, cs[a.slot]).then_inc(ctx_turned, 1)
                if b:
                    pe.wait_ge(rdenw_ready, b.n + 1)
                    wait(pe, x1_ready, b.n)
                    turn_tiles(pRdenT, rdenw).then_inc(rden_turned, 1)
                if a:
                    pe.wait_ge(expq_ready, a.n + 1)
                    wait(pe, rden_ready, a.n)
                    for t in range(HT):
                        i = pe.matmul(pDen[:, t * HEADS:(t + 1) * HEADS], expq[a.slot][:, t * P:(t + 1) * P], headsel[:, :],
                                      start=True, stop=True)
                    i.then_inc(den_done, 1)
                    pe.wait_ge(expk_ready, a.n + 1)
                    pe.wait_ge(ctxT_ready, a.n + 1)
                    turn_tiles(pExpkT, expk).then_inc(expk_turned, 1)
                if b:
                    pe.wait_ge(kvs_ready, b.n + 1)
                    pe.wait_ge(softq_ready, b.n + 1)
                    for h in range(2):
                        i = pe.matmul(pAttn[:, h * WIDE:(h + 1) * WIDE], kvs[:, :], expq[b.slot][:, h * WIDE:(h + 1) * WIDE],
                                      start=True, stop=True)
                    i.then_inc(attn_done, 1)
                if a:
                    pe.wait_ge(expkT_ready, a.n + 1)
                    wait(pe, kvs_ready, a.n)
                    for t in range(HT):
                        i = pe.matmul(pKV, expkT[:, t * P:(t + 1) * P], ctxT[:, t * P:(t + 1) * P],
                                      start=(t == 0), stop=(t == HT - 1))
                    i.then_inc(kv_done, 1)
                if c:
                    pe.wait_ge(x2_ready, c.n + 1)
                    wait(pe, xl_ready, c.n)
                    turn_tiles(pX2T, x2).then_inc(x2_turned, 1)

            pe.wait_ge(consts_ready, NCONST)
            mixer(pe, mixer_turn, 2)

            def products(dst, par, g, tb):
                for t in range(HT):
                    hi, lo = (wgu[:, par, q, g, t * P:(t + 1) * P] for q in range(2))
                    pe.matmul(dst, hi, xh[:, tb, t, :], start=(t == 0), stop=False)
                    pe.matmul(dst, hi, xl[:, tb, t, :], start=False, stop=False)
                    i = pe.matmul(dst, lo, xh[:, tb, t, :], start=False, stop=(t == HT - 1))
                return i

            def gate(c, par, tb):
                pe.wait_ge(blocks_done, c * TB + tb + 1)
                if tb == 0:
                    pe.wait_ge(wl_ready, c * 2 + 1)
                products(banks[tb][:, 0, :], par, 0, tb).then_inc(gate_done, 1)

            def up(c, par, tb):
                if tb == 0:
                    pe.wait_ge(wl_ready, c * 2 + 2)
                products(banks[tb][:, 1, :], par, 1, tb).then_inc(up_done, 1)

            def chunk(c, par, first=0):
                for tb in range(first, TB):
                    gate(c, par, tb)
                    up(c, par, tb)

            pe.wait_ge(xl_ready, QT)
            pe.wait_ge(expkT_ready, B)
            pe.wait_ge(fwl_ready, SLICES)
            gate(0, 0, 0)
            mixer_turn(LOOPS, XS + 1)
            up(0, 0, 0)
            pe.wait_ge(rden_ready, B)
            pe.wait_ge(kvs_ready, B)
            pe.wait_ge(x1_ready, B)
            pe.wait_ge(xl_ready, B)
            chunk(0, 0, 1)
            with pe.Fori(0, PAIRS) as p:
                for j in range(2):
                    chunk(p * 2 + (1 + j), 1 - j)
            for tb in range(TB):
                pe.wait_ge(blocks_done, FULL * TB + tb + 1)
                pe.wait_ge(wl_ready, GU)
                products(banks[tb][:, 0, :], 1, 0, tb).then_inc(gate_done, 1)

            def tile(g, slot, half, first=False, k0=0):
                pe.wait_ge(il_ready, g + 1)
                wait(pe, y_ready, g - 1)
                dst = banks[slot][:, 0, :]
                for k in range(k0, KT):
                    if first:
                        pe.wait_ge(wdl_ready, half * KT + k + 1)
                    h, l = (v[slot][:, k * P:(k + 1) * P] for v in (ih, il))
                    if k < FULL:
                        pe.matmul(dst, h, wdh[:, k, :], start=(k == 0), stop=False)
                        pe.matmul(dst, h, wdl[:, k, :], start=False, stop=False)
                        i = pe.matmul(dst, l, wdh[:, k, :], start=False, stop=False)
                    else:
                        pe.matmul(dst, h, wdh[:, k, :], start=False, stop=False)
                        i = pe.matmul(dst, h, wdl[:, k, :], start=False, stop=True)
                    i.then_inc(down_step, k0 + 1 if k == k0 else 1)

            def first_part(t):
                dst, h, l = banks[t][:, 0, :], ih[t], il[t]
                pe.wait_ge(blocks_done, FULL * TB + TB + t + 1)
                pe.wait_ge(ih_first, t + 1)
                for k in range(FS):
                    if t == 0:
                        pe.wait_ge(wdl_ready, k + 1)
                    pe.matmul(dst, h[:, k * P:(k + 1) * P], wdh[:, k, :], start=(k == 0), stop=False)
                    pe.matmul(dst, h[:, k * P:(k + 1) * P], wdl[:, k, :], start=False, stop=False)
                pe.wait_ge(il_first, t + 1)
                for k in range(FS):
                    pe.matmul(dst, l[:, k * P:(k + 1) * P], wdh[:, k, :], start=False, stop=False)

            for t in range(2):
                first_part(t)
            for t in range(2):
                tile(t, t, 0, t == 0, FS)
            for half in range(2):
                g0 = half * TT
                if half:
                    tile(g0, 0, half, True)
                    tile(g0 + 1, 1, half)
                with pe.Fori(0, TT // 2 - 1) as q:
                    for s in range(2):
                        tile(q * 2 + (g0 + 2 + s), s, half)


def kernel(x, ctx_4096, L0_ffn_gate_codes, L0_ffn_gate_scales, L0_ffn_up_codes, L0_ffn_up_scales,
           L0_ffn_down_codes, L0_ffn_down_scales):
    import numpy as np
    import concourse.bacc as bacc
    from concourse.bass_utils import run_bass_kernel_spmd as run

    x, ctx = np.ascontiguousarray(x), np.ascontiguousarray(ctx_4096)
    I, H = L0_ffn_gate_codes.shape
    full, half = I // P, I % P

    def turned(codes, scales, a, b):
        c = np.asarray(codes)[a:b].T.reshape(H // P, P, b - a).transpose(1, 0, 2)
        s = np.asarray(scales)[a:b].T.reshape(H // P, 2, b - a).transpose(1, 0, 2)
        return c, s

    gu_c, gu_s = [], []
    for c in range(full):
        for codes, scales in ((L0_ffn_gate_codes, L0_ffn_gate_scales), (L0_ffn_up_codes, L0_ffn_up_scales)):
            a, b = turned(codes, scales, c * P, (c + 1) * P)
            gu_c.append(a.reshape(P, H))
            gu_s.append(b.reshape(2, H))
    g, u = (turned(codes, scales, full * P, I) for codes, scales in
            ((L0_ffn_gate_codes, L0_ffn_gate_scales), (L0_ffn_up_codes, L0_ffn_up_scales)))
    gu_c.append(np.concatenate([g[0], u[0]], axis=2).reshape(P, H))
    gu_s.append(np.concatenate([g[1], u[1]], axis=2).reshape(2, H))

    dc, ds = np.asarray(L0_ffn_down_codes).T, np.asarray(L0_ffn_down_scales).T
    d_c = np.concatenate([dc, dc[full * P:]]).reshape(full + 1, P, H)
    d_s = np.concatenate([ds, ds[2 * full:]]).reshape(full + 1, 2, H)

    arrays = {"x": x, "ctx": ctx, "gu_codes": np.stack(gu_c), "gu_scales": np.stack(gu_s),
              "d_codes": d_c, "d_scales": d_s}
    nc = bacc.Bacc("TRN2", target_bir_lowering=False, num_devices=1, dynamic_dma_scratch_size=1024)
    args, ins = [], {}
    for name, a in arrays.items():
        ins[f"in_{name}"] = np.ascontiguousarray(a)
        args.append(nc.dram_tensor(f"in_{name}", a.shape, mybir.dt.from_np(a.dtype), kind="ExternalInput").ap())
    out = nc.dram_tensor("out_y", x.shape, F32, kind="ExternalOutput").ap()
    xattn_ffn(nc, *args, out)
    r = run(nc, [ins], core_ids=[0])
    return r.results[0]["out_y"]
```
